# Optimizing a Trainium2 kernel written in Bass

```python
import numpy as np
import jax
import jax.numpy as jnp

def _softmax(x, axis=-1):
    return jax.nn.softmax(x, axis=axis)

def _gelu(x):
    return jax.nn.gelu(x, approximate=True)

def _silu(x):
    return jax.nn.silu(x)

def _sigmoid(x):
    return jax.nn.sigmoid(x)

def _layernorm(x, axis=-1, eps=1e-05):
    m = jnp.mean(x, axis=axis, keepdims=True)
    v = jnp.var(x, axis=axis, keepdims=True)
    return (x - m) / jnp.sqrt(v + eps)

def _scatter_add(tgt, idx, src, axis=0):
    return tgt.at[idx].add(src)

def _segment_sum(src, seg, n):
    return jax.ops.segment_sum(src, seg, n)
kernel_name = 'mk_gnn_resnorm_d1_gnn_r8_53576c'

def setup_inputs(seed: int=0):
    np.random.seed(seed)
    _w = jnp.asarray

    def _rec_inputs():
        import jax
        import jax.numpy as jnp
        _gk = jax.random.key(seed)
        x = -0.0003713 + 1 * jax.random.normal(jax.random.fold_in(_gk, 1), (6250, 128), jnp.float32)
        src = jax.random.randint(jax.random.fold_in(_gk, 2), (200000,), 0, 6250, jnp.int32)
        dst = jnp.minimum((6250 * jax.random.uniform(jax.random.fold_in(_gk, 3), (200000,)) ** 2.0).astype(jnp.int32), 49999)
        _o = jnp.argsort(dst, stable=True)
        src = src[_o]
        dst = dst[_o]
        edge_attr_128 = 2.93046e-05 + 1.00006 * jax.random.normal(jax.random.fold_in(_gk, 12), (200000, 128), jnp.float32)
        return (x, src, dst, edge_attr_128)
    x, src, dst, edge_attr_128 = _rec_inputs()

    def _L0_gnn_setup():
        import jax, jax.numpy as jnp
        import numpy as np
        N = 12500
        E = 80000
        V_IN = 128
        U_IN = 64
        HID = 128
        B = 128
        key = jax.random.key(seed)
        ks = jax.random.split(key, 9)
        x = jax.random.normal(ks[0], (N, V_IN), dtype=jnp.float32)
        edge_index = jax.random.randint(ks[1], (2, E), 0, N, dtype=jnp.int64)
        edge_attr = jax.random.normal(ks[2], (E, HID), dtype=jnp.float32)
        u = jax.random.normal(ks[3], (B, U_IN), dtype=jnp.float32)
        batch = jnp.sort(jax.random.randint(ks[4], (N,), 0, B, dtype=jnp.int64))
        fan_in1 = V_IN + HID + U_IN
        W1 = jax.random.normal(ks[5], (fan_in1, HID), dtype=jnp.float32) / np.sqrt(fan_in1)
        b1 = jnp.zeros((HID,), dtype=jnp.float32)
        W2 = jax.random.normal(ks[6], (HID, HID), dtype=jnp.float32) / np.sqrt(HID)
        b2 = jnp.zeros((HID,), dtype=jnp.float32)
        return {'x': x, 'edge_index': edge_index, 'edge_attr': edge_attr, 'u': u, 'batch': batch, 'W1': W1, 'b1': b1, 'W2': W2, 'b2': b2}
    _L0_gnn_all = _L0_gnn_setup()
    _L0_gnn_in = {k: v for k, v in _L0_gnn_all.items() if k in ('u', 'W1', 'b1', 'W2', 'b2')}
    del _L0_gnn_all
    return {'x': x, 'src': src, 'dst': dst, 'edge_attr_128': edge_attr_128, 'L0_gnn_u': _L0_gnn_in['u'], 'L0_gnn_W1': _L0_gnn_in['W1'], 'L0_gnn_b1': _L0_gnn_in['b1'], 'L0_gnn_W2': _L0_gnn_in['W2'], 'L0_gnn_b2': _L0_gnn_in['b2']}

def reference(x, src, dst, edge_attr_128, L0_gnn_u, L0_gnn_W1, L0_gnn_b1, L0_gnn_W2, L0_gnn_b2):
    import jax
    import jax.numpy as jnp

    def _L0_gnn_ref(x, edge_index, edge_attr, u, batch, W1, b1, W2, b2):
        import jax, jax.numpy as jnp
        import numpy as np
        N = 12500
        E = 80000
        V_IN = 128
        U_IN = 64
        HID = 128
        B = 128
        col = edge_index[1]
        agg = jax.ops.segment_sum(edge_attr, col, num_segments=x.shape[0])
        h = jnp.concatenate([x, agg, u[batch]], axis=1)
        h = jax.nn.relu(h @ W1 + b1)
        return h @ W2 + b2
    edge_index = jnp.stack([src, dst])
    batch0 = jnp.zeros((6250,), jnp.int32)
    x = _layernorm(x + _L0_gnn_ref(x, edge_index, edge_attr_128, L0_gnn_u, batch0, L0_gnn_W1, L0_gnn_b1, L0_gnn_W2, L0_gnn_b2), axis=-1)
    return x

_drawn_inputs = setup_inputs


def setup_inputs(seed=0):
    import zlib

    import numpy as np

    out = dict(_drawn_inputs(seed))
    spreads = {'L0_gnn_b1': (0.0, 0.1), 'L0_gnn_b2': (0.0, 0.1)}
    factors = {}
    for name, (base, spread) in spreads.items():
        noise = np.random.default_rng([zlib.crc32(name.encode()), seed]).standard_normal(out[name].shape)
        drawn = base * np.exp(spread * noise) if base else spread * noise
        out[name] = jnp.asarray(drawn.astype(out[name].dtype))
    for name, factor in factors.items():
        out[name] = (out[name] * factor).astype(out[name].dtype)
    return out
```

```python
import concourse.bass as bass
from concourse import mybir
from contextlib import ExitStack

F32 = mybir.dt.float32
I32 = mybir.dt.int32
ALU = mybir.AluOpType
ACT = mybir.ActivationFunctionType
AX = mybir.AxisListType

P = 128
EPS = 1e-5
RUN = 2
WIN = RUN * P
SPAN = 32
TILES = P // SPAN
COLS = 96
GROUPS = 2
WINS = GROUPS * TILES
STEP = WINS * WIN
SLOTS = 8
PAD = 1 << 20


def residual_gnn_layer(nc, x, dst, edge_attr, u, w1, b1, w2, b2, out):
    nodes, feats = x.shape
    edges = edge_attr.shape[0]
    ufeats = u.shape[1]
    full = edges // STEP
    steps = full + 1
    rest = edges - full * STEP
    rest_wins = rest // WIN
    rest_parts = (rest - rest_wins * WIN) // RUN
    assert feats == P and steps <= P and rest and rest % RUN == 0 and PAD > nodes
    rounds = full // SLOTS
    assert full == rounds * SLOTS + 1
    sweeps = -(-nodes // SPAN)
    pair = 2 * P
    blocks = nodes // pair
    last_parts = (nodes - blocks * pair) // 2
    assert nodes == blocks * pair + 2 * last_parts and last_parts
    early = blocks // rounds
    assert early * rounds == blocks and early <= SLOTS // 2
    width = nodes + COLS + SPAN

    edge_full = edge_attr[0:full * STEP, :].rearrange("(s w p r) f -> s p w (r f)", w=WINS, p=P, r=RUN)
    edge_rest = edge_attr[full * STEP:full * STEP + rest_wins * WIN, :].rearrange("(w p r) f -> p w (r f)", p=P, r=RUN)
    edge_last = edge_attr[full * STEP + rest_wins * WIN:edges, :].rearrange("(p r) f -> p (r f)", r=RUN)
    x_full = x[0:blocks * pair, :].rearrange("(b p r) f -> p b (r f)", p=P, r=2)
    x_last = x[blocks * pair:nodes, :].rearrange("(p r) f -> p (r f)", r=2)
    out_full = out[0:blocks * pair, :].rearrange("(b p r) f -> p b (r f)", p=P, r=2)
    out_last = out[blocks * pair:nodes, :].rearrange("(p r) f -> p (r f)", r=2)

    ctx = ExitStack()
    with ctx:
        def sb(name, shape, dt=F32):
            return ctx.enter_context(nc.sbuf_tensor(name, shape, dt))

        def pb(name, shape):
            return ctx.enter_context(nc.psum_tensor(name, shape, F32))

        def sem(name):
            return ctx.enter_context(nc.semaphore(name))

        slots = sb("slots", [P, SLOTS, WINS, RUN * feats])
        tail = sb("tail", [P, WINS, RUN * feats])
        dst_int = sb("dst_int", [steps, WINS, WIN], I32)
        dst_f = sb("dst_f", [steps, WINS, WIN])
        dst_real = sb("dst_real", [steps, WINS, WIN])
        low = sb("low", [steps, WINS])
        high = sb("high", [steps, WINS])
        group_low = sb("group_low", [steps, GROUPS])
        group_high = sb("group_high", [steps, GROUPS])
        bad = sb("bad", [steps, 4, WINS])
        bad_count = sb("bad_count", [steps, 1])
        good = sb("good", [P, 1])
        offset = sb("offset", [steps, WINS])
        row_src = sb("row_src", [steps, GROUPS, TILES, SPAN])
        flag = sb("flag", [1, 1], I32)
        bases = sb("bases", [1, GROUPS, steps], I32)
        edge_node = sb("edge_node", [P, steps, WINS * RUN])
        row_node = sb("row_node", [P, steps, GROUPS])
        iota_int = sb("iota_int", [P, P], I32)
        iota = sb("iota", [P, P])
        iota_span = sb("iota_span", [P, SPAN])
        ident = sb("ident", [P, P])
        ones = sb("ones", [P, P])
        hot = [sb(f"hot{i}", [P, WINS * RUN, SPAN]) for i in range(2)]
        row_hot = [sb(f"row_hot{i}", [P, GROUPS, COLS]) for i in range(2)]
        rows = [sb(f"rows{i}", [P, GROUPS, feats]) for i in range(2)]
        agg_t = sb("agg_t", [P, width])
        x_sb = sb("x_sb", [P, blocks + 1, pair])
        x_t = sb("x_t", [P, blocks + 1, pair])
        w1x = sb("w1x", [P, feats])
        w1a = sb("w1a", [P, feats])
        w1u = sb("w1u", [ufeats, feats])
        w2_sb = sb("w2_sb", [P, feats])
        u_col = sb("u_col", [ufeats, 1])
        b1_col = sb("b1_col", [P, 1])
        bias = sb("bias", [P, 1])
        b2_row = sb("b2_row", [1, feats])
        b2_all = sb("b2_all", [P, feats])
        z = x_sb[:, :, :].rearrange("p b (r f) -> p b r f", r=2)
        hid = [sb(f"hid{i}", [P, pair]) for i in range(2)]
        total = sb("total", [P, blocks + 1, 2])
        neg_mean = sb("neg_mean", [P, blocks + 1, 2])
        squares = sb("squares", [P, blocks + 1, 2])
        scratch = sb("scratch", [P, 2, feats])
        var_eps = sb("var_eps", [P, blocks + 1, 2])
        minus_half = sb("minus_half", [P, 2])
        rstd = sb("rstd", [P, blocks + 1, 2])
        shift = sb("shift", [P, blocks + 1, 2])

        rows_ps = [pb(f"rows_ps{i}", [P, GROUPS, 256]) for i in range(2)]
        cols_ps = [pb(f"cols_ps{i}", [P, GROUPS, 256]) for i in range(2)]
        t_ps = [pb(f"t_ps{i}", [P, 4, P]) for i in range(2)]
        hid_ps = pb("hid_ps", [P, 512])
        y_ps = pb("y_ps", [P, 2, 256])

        edges_in = [sem(f"edges_in{j}") for j in range(SLOTS)]
        tail_zero = sem("tail_zero")
        tail_in = sem("tail_in")
        dst_pad = sem("dst_pad")
        dst_in = sem("dst_in")
        x_in = sem("x_in")
        w_in = sem("w_in")
        iota_made = sem("iota_made")
        ident_made = sem("ident_made")
        ones_made = sem("ones_made")
        agg_zero = sem("agg_zero")
        prep = sem("prep")
        bad_counted = sem("bad_counted")
        bad_summed = sem("bad_summed")
        flag_made = sem("flag_made")
        local_made = sem("local_made")
        row_src_made = sem("row_src_made")
        ids_turned = sem("ids_turned")
        ids_copied = sem("ids_copied")
        bases_turned = sem("bases_turned")
        bases_made = sem("bases_made")
        u_done = sem("u_done")
        bias_made = sem("bias_made")
        b2_spread = sem("b2_spread")
        b2_made = sem("b2_made")
        hot_made = sem("hot_made")
        row_hot_made = sem("row_hot_made")
        level1_done = sem("level1_done")
        rows_copied = sem("rows_copied")
        level2_done = sem("level2_done")
        added0 = sem("added0")
        added1 = sem("added1")
        x_turned = sem("x_turned")
        x_copied = sem("x_copied")
        x_plus_b2 = sem("x_plus_b2")
        hid_done = sem("hid_done")
        hid_made = sem("hid_made")
        y_done = sem("y_done")
        z_made = sem("z_made")
        stats_clear = sem("stats_clear")
        mean_made = sem("mean_made")
        squares_made = sem("squares_made")
        eps_added = sem("eps_added")
        half_made = sem("half_made")
        rstd_made = sem("rstd_made")
        shift_made = sem("shift_made")
        normed = sem("normed")
        out_stored = sem("out_stored")

        block = ctx.enter_context(nc.Block())

        def wait_some(eng, signal, count):
            if not isinstance(count, int) or count > 0:
                eng.wait_ge(signal, count)

        def block_parts(b):
            return P if b < blocks else last_parts

        def more_sweeps(eng, sweep):
            eng.wait_ge(flag_made, 1)
            enough = eng.value_load(flag[0:1, 0:1], min_val=0, max_val=1)
            with eng.If(enough < 1):
                with eng.Fori(1, sweeps) as k:
                    sweep(k)

        def fills(j):
            return rounds + (1 if j == 0 else 0)

        @block.sync
        def _(sp):
            def load(j, s):
                sp.dma_start(slots[:, j, :, :], edge_full[s]).then_inc(edges_in[j], 16)

            def sweep(k):
                if not isinstance(k, int):
                    sp.wait_ge(level1_done, k * steps)
                for j in range(SLOTS):
                    load(j, j)
                with sp.Fori(0, rounds - 1) as r:
                    for j in range(SLOTS):
                        sp.wait_ge(level1_done, r * SLOTS + (j + 1) + k * steps)
                        load(j, (r + 1) * SLOTS + j)
                sp.wait_ge(level1_done, k * steps + (full - SLOTS))
                load(0, full - 1)

            sp.wait_ge(dst_pad, 1)
            sp.dma_start(dst_int[0:full, :, :], dst[0:full * STEP].rearrange("(s w e) -> s w e", w=WINS, e=WIN)).then_inc(dst_in, 16)
            sp.dma_start(dst_int[full:steps, :, :].rearrange("s w e -> s (w e)")[:, 0:rest],
                         dst[full * STEP:edges].rearrange("(s e) -> s e", s=1)).then_inc(dst_in, 16)
            sweep(0)
            sp.wait_ge(tail_zero, 1)
            if rest_wins:
                sp.dma_start(tail[:, 0:rest_wins, :], edge_rest).then_inc(tail_in, 16)
            if rest_parts:
                sp.dma_start(tail[0:rest_parts, rest_wins, :], edge_last).then_inc(tail_in, 16)
            more_sweeps(sp, sweep)

        tail_loads = 16 * (bool(rest_wins) + bool(rest_parts))

        @block.gpsimd
        def _(pool):
            nc.gpsimd.memset(dst_int[:, :, :], PAD).then_inc(dst_pad, 1)
            nc.gpsimd.iota(iota_int[:, :], [[1, P]], base=0, channel_multiplier=0).then_inc(iota_made, 1)
            nc.gpsimd.memset(ones[:, :], 1.0).then_inc(ones_made, 1)
            pool.wait_ge(ones_made, 1)
            nc.gpsimd.affine_select(out=ident[:, :], in_=ones[:, :], compare_op=ALU.is_equal, fill=0.0,
                                    base=0, pattern=[[-1, P]], channel_multiplier=1).then_inc(ident_made, 1)
            nc.gpsimd.memset(agg_t[:, :], 0.0).then_inc(agg_zero, 1)
            nc.gpsimd.memset(tail[:, :, :], 0.0).then_inc(tail_zero, 1)
            nc.gpsimd.memset(minus_half[:, :], -0.5).then_inc(half_made, 1)
            pool.wait_ge(x_in, 32)
            pool.wait_ge(b2_made, 1)

            def add_b2(b):
                n = P if not isinstance(b, int) else block_parts(b)
                pool.wait_ge(x_turned, b + 1)
                xv = x_sb[0:n, bass.ds(b, 1), :].rearrange("p o (r f) -> p (o r) f", r=2)
                nc.gpsimd.tensor_tensor(xv, xv, b2_all[0:n, :].unsqueeze(1).broadcast_to([n, 2, feats]),
                                        ALU.add).then_inc(x_plus_b2, 1)
            with pool.Fori(0, blocks) as b:
                add_b2(b)
            add_b2(blocks)
            for b in range(1):
                pool.wait_ge(eps_added, 1)
                nc.gpsimd.tensor_tensor(rstd[:, :, :], var_eps[:, :, :],
                                        minus_half[:, 0:1].unsqueeze(1).broadcast_to([P, blocks + 1, 2]),
                                        ALU.pow).then_inc(rstd_made, 1)

        @block.scalar
        def _(act):
            act.dma_start(w1x[:, :], w1[0:feats, :]).then_inc(w_in, 16)
            act.dma_start(w1a[:, :], w1[feats:2 * feats, :]).then_inc(w_in, 16)
            act.dma_start(w1u[:, :], w1[2 * feats:2 * feats + ufeats, :]).then_inc(w_in, 16)
            act.dma_start(w2_sb[:, :], w2).then_inc(w_in, 16)
            act.dma_start(u_col[:, :], u[0:1, :].rearrange("a c -> c a")).then_inc(w_in, 16)
            act.dma_start(b1_col[:, :], b1.rearrange("(c a) -> c a", a=1)).then_inc(w_in, 16)
            act.dma_start(b2_row[:, :], b2.rearrange("(a c) -> a c", a=1)).then_inc(w_in, 16)
            act.dma_start(x_sb[:, 0:blocks, :], x_full).then_inc(x_in, 16)
            act.dma_start(x_sb[0:last_parts, blocks, :], x_last).then_inc(x_in, 16)
            act.wait_ge(u_done, 1)
            nc.scalar.activation(bias[:, :], hid_ps[:, 0:1], ACT.Identity, bias=b1_col[:, :]).then_inc(bias_made, 1)
            act.wait_ge(b2_spread, 1)
            nc.scalar.activation(b2_all[:, :], y_ps[:, 0, 0:feats], ACT.Copy).then_inc(b2_made, 1)

            def copy_rows(i, s, k):
                act.wait_ge(level1_done, k * steps + (s + 1))
                if not (isinstance(s, int) and isinstance(k, int) and s < 2):
                    act.wait_ge(level2_done, k * steps + (s - 1))
                nc.scalar.activation(rows[i][:, :, :], rows_ps[i][:, :, 0:feats], ACT.Copy).then_inc(rows_copied, 1)

            def copy_x(b):
                act.wait_ge(x_turned, b + 1)
                n = P if not isinstance(b, int) else block_parts(b)
                o = x_t[:, bass.ds(b, 1), 0:2 * n].rearrange("f o (p r) -> f (o r) p", r=2)
                nc.scalar.activation(o, hid_ps[:, 0:2 * n].rearrange("f (r p) -> f r p", r=2), ACT.Copy).then_inc(x_copied, 1)

            def sweep(k):
                first = isinstance(k, int)
                for i in range(2):
                    copy_rows(i, i, k)
                    if first and i == 1:
                        pass
                for i in range(2, SLOTS):
                    copy_rows(i % 2, i, k)
                    if first and i % 4 == 1 and (i - 1) // 4 - 1 < 0:
                        pass
                with act.Fori(1, rounds) as r:
                    for j in range(SLOTS):
                        copy_rows(j % 2, r * SLOTS + j, k)
                copy_rows((full - 1) % 2, full - 1, k)
                copy_rows(full % 2, full, k)

            act.wait_ge(bias_made, 1)
            with act.Fori(0, blocks) as b:
                copy_x(b)
            copy_x(blocks)
            sweep(0)
            more_sweeps(act, sweep)

            def relu(b):
                i = 0
                act.wait_ge(hid_done, b + 1)
                n = P if not isinstance(b, int) else block_parts(b)
                wait_some(act, y_done, b)
                nc.scalar.activation(hid[i][:, 0:2 * n], hid_ps[:, 0:2 * n], ACT.Relu, bias=bias[:, :]).then_inc(hid_made, 1)

            def square(b):
                n = P if not isinstance(b, int) else block_parts(b)
                act.wait_ge(mean_made, b + 1)
                wait_some(act, squares_made, b)
                for r in range(2):
                    last = nc.scalar.activation(scratch[0:n, r, :], z[0:n, bass.ds(b, 1), r, :].rearrange("p o f -> p (o f)"), ACT.Square,
                                                bias=neg_mean[0:n, bass.ds(b, 1), r], accum_out=squares[0:n, bass.ds(b, 1), r])
                last.then_inc(squares_made, 1)
            act.wait_ge(stats_clear, 1)
            relu(0)
            square(0)
            with act.Fori(1, blocks) as b:
                relu(b)
                square(b)
            relu(blocks)
            square(blocks)

            def normalise(b):
                n = P if not isinstance(b, int) else block_parts(b)
                for r in range(2):
                    last = nc.scalar.activation(z[0:n, bass.ds(b, 1), r, :], z[0:n, bass.ds(b, 1), r, :], ACT.Identity,
                                                scale=rstd[0:n, bass.ds(b, 1), r], bias=shift[0:n, bass.ds(b, 1), r])
                last.then_inc(normed, 1)
            act.wait_ge(rstd_made, 1)
            act.wait_ge(shift_made, 1)
            with act.Fori(0, blocks) as b:
                normalise(b)
                act.wait_ge(normed, b + 1)
                act.dma_start(out_full[:, bass.ds(b, 1), :], z[:, bass.ds(b, 1), :, :].rearrange("p o r f -> p o (r f)")).then_inc(out_stored, 16)
            normalise(blocks)
            act.wait_ge(normed, blocks + 1)
            act.dma_start(out_last, z[0:last_parts, blocks, :, :].rearrange("p r f -> p (r f)")).then_inc(out_stored, 16)
            act.wait_ge(out_stored, 16 * (blocks + 1))

        @block.vector
        def _(dve):
            V = nc.vector
            count = [0]

            def then(ins):
                count[0] += 1
                ins.then_inc(prep, 1)
                dve.wait_ge(prep, count[0])

            dve.wait_ge(iota_made, 1)
            V.tensor_copy(iota[:, :], iota_int[:, :]).then_inc(iota_made, 1)
            V.tensor_copy(iota_span[:, :], iota_int[:, 0:SPAN]).then_inc(iota_made, 1)
            dve.wait_ge(iota_made, 3)
            dve.wait_ge(dst_in, 32)
            then(V.tensor_copy(dst_f[:, :, :], dst_int[:, :, :]))
            V.tensor_reduce(low[:, :], dst_f[:, :, :], AX.X, ALU.min)
            then(V.scalar_tensor_tensor(dst_real[:, :, :], dst_f[:, :, :], float(PAD), dst_f[:, :, :], ALU.is_lt, ALU.mult))
            then(V.tensor_reduce(high[:, :], dst_real[:, :, :], AX.X, ALU.max))
            then(V.tensor_scalar(bad[:, 0, :], low[:, :], 0.0, None, ALU.is_lt))
            then(V.tensor_scalar(low[:, :], low[:, :], float(nodes - 1), None, ALU.min))
            V.tensor_reduce(group_low[:, :], low[:, :].rearrange("s (g t) -> s g t", g=GROUPS), AX.X, ALU.min)
            V.tensor_reduce(group_high[:, :], high[:, :].rearrange("s (g t) -> s g t", g=GROUPS), AX.X, ALU.max)
            V.tensor_scalar(bad[:, 1, :], high[:, :], float(nodes), None, ALU.is_ge)
            then(V.tensor_tensor(bad[:, 2, :], high[:, :], low[:, :], ALU.subtract))
            V.tensor_scalar(bad[:, 2, :], bad[:, 2, :], float(SPAN), None, ALU.is_ge)
            V.memset(bad[:, 3, :], 0.0)
            then(V.tensor_tensor(group_high[:, :], group_high[:, :], group_low[:, :], ALU.subtract))
            then(V.tensor_scalar(bad[:, 3, 0:GROUPS], group_high[:, :], float(COLS), None, ALU.is_ge))
            V.tensor_reduce(bad_count[:, :], bad[:, :, :], AX.XY, ALU.add).then_inc(bad_counted, 1)
            dve.wait_ge(bad_summed, 1)
            then(V.tensor_scalar(good[:, :], t_ps[0][:, 0, 0:1], 0.0, None, ALU.is_equal))
            V.tensor_copy(flag[:, :], good[0:1, :]).then_inc(flag_made, 1)
            V.tensor_scalar(low[:, :], low[:, :], good[0:steps, :], None, ALU.mult)
            then(V.tensor_scalar(group_low[:, :], group_low[:, :], good[0:steps, :], None, ALU.mult))
            V.tensor_tensor(offset[:, :].rearrange("s (g t) -> s g t", g=GROUPS), low[:, :].rearrange("s (g t) -> s g t", g=GROUPS),
                            group_low[:, :].unsqueeze(2).broadcast_to([steps, GROUPS, TILES]), ALU.subtract)
            then(V.tensor_tensor(dst_real[:, :, :], dst_f[:, :, :], low[:, :].unsqueeze(2).broadcast_to([steps, WINS, WIN]), ALU.subtract))
            V.tensor_tensor(row_src[:, :, :, :].rearrange("s g t j -> s (g t) j"),
                            offset[:, :].unsqueeze(2).broadcast_to([steps, WINS, SPAN]),
                            iota[0:steps, 0:SPAN].unsqueeze(1).broadcast_to([steps, WINS, SPAN]), ALU.add).then_inc(local_made, 1)
            for q in range(WINS * RUN // 4):
                dve.wait_ge(ids_turned, q + 1)
                V.tensor_copy(edge_node[:, :, 4 * q:4 * q + 4].rearrange("p s c -> p c s"), t_ps[q % 2][:, :, 0:steps]).then_inc(ids_copied, 1)
            dve.wait_ge(bases_turned, 1)
            V.tensor_copy(row_node[:, :, :].rearrange("p s g -> p g s"), t_ps[0][:, 0:GROUPS, 0:steps])
            V.tensor_copy(bases[:, :, :], t_ps[1][0:1, 0:GROUPS, 0:steps]).then_inc(bases_made, 1)
            dve.wait_ge(bases_made, 1)
            dve.wait_ge(agg_zero, 1)

            def make_hot(i, s, k):
                known = isinstance(s, int) and isinstance(k, int)
                if not (known and s < 2):
                    dve.wait_ge(level1_done, k * steps + (s - 1))
                V.tensor_tensor(hot[i][:, :, :],
                                edge_node[:, bass.ds(s, 1), :].rearrange("p o c -> p (o c)").unsqueeze(2).broadcast_to([P, WINS * RUN, SPAN]),
                                iota_span[:, :].unsqueeze(1).broadcast_to([P, WINS * RUN, SPAN]), ALU.is_equal).then_inc(hot_made, 1)
                if not (known and s < 2):
                    dve.wait_ge(level2_done, k * steps + (s - 1))
                V.tensor_tensor(row_hot[i][:, :, :],
                                row_node[:, bass.ds(s, 1), :].rearrange("p o g -> p (o g)").unsqueeze(2).broadcast_to([P, GROUPS, COLS]),
                                iota[:, 0:COLS].unsqueeze(1).broadcast_to([P, GROUPS, COLS]), ALU.is_equal).then_inc(row_hot_made, 1)

            def add_cols(i, s, k):
                dve.wait_ge(level2_done, k * steps + (s + 1))
                known = isinstance(s, int) and isinstance(k, int)
                for g, (mine, other) in enumerate(((added0, added1), (added1, added0))):
                    if isinstance(k, int):
                        base = dve.value_load(bases[0:1, g, bass.ds(s, 1)], min_val=0, max_val=nodes - 1)
                    else:
                        base = k * SPAN
                    at = agg_t[:, bass.ds(base, COLS)]
                    if not (known and s == 0 and g == 0):
                        dve.wait_ge(other, k * steps + (s + g))
                    V.tensor_tensor(at, at, cols_ps[i][:, g, 0:COLS], ALU.add).then_inc(mine, 1)

            def sweep(k):
                if not isinstance(k, int):
                    dve.wait_ge(hot_made, k * steps)
                    V.tensor_scalar(iota_span[:, :], iota_span[:, :], float(SPAN), None, ALU.add).then_inc(iota_made, 1)
                    dve.wait_ge(iota_made, k + 3)
                make_hot(0, 0, k)
                make_hot(1, 1, k)
                add_cols(0, 0, k)
                for j in range(1, SLOTS):
                    make_hot((j + 1) % 2, j + 1, k)
                    add_cols(j % 2, j, k)
                with dve.Fori(1, rounds) as r:
                    for j in range(SLOTS):
                        make_hot((j + 1) % 2, r * SLOTS + (j + 1), k)
                        add_cols(j % 2, r * SLOTS + j, k)
                make_hot(full % 2, full, k)
                add_cols((full - 1) % 2, full - 1, k)
                add_cols(full % 2, full, k)

            sweep(0)
            more_sweeps(dve, sweep)

            def residual(b):
                n = P if not isinstance(b, int) else block_parts(b)
                dve.wait_ge(y_done, b + 1)
                dve.wait_ge(x_plus_b2, b + 1)
                for r in range(2):
                    last = V.scalar_tensor_tensor(z[0:n, bass.ds(b, 1), r, :].rearrange("p o f -> p (o f)"), y_ps[0:n, r, 0:feats], 1.0,
                                                  z[0:n, bass.ds(b, 1), r, :].rearrange("p o f -> p (o f)"), ALU.mult, ALU.add,
                                                  accum_out=total[0:n, bass.ds(b, 1), r])
                last.then_inc(z_made, 1)
                dve.wait_ge(z_made, b + 1)
                V.tensor_scalar(neg_mean[0:n, bass.ds(b, 1), :], total[0:n, bass.ds(b, 1), :], -1.0 / feats, None, ALU.mult).then_inc(mean_made, 1)

            V.memset(squares[:, blocks, :], 1.0)
            then(V.memset(neg_mean[:, blocks, :], 0.0))
            V.memset(total[:, blocks, :], 0.0).then_inc(stats_clear, 1)
            dve.wait_ge(stats_clear, 1)
            with dve.Fori(0, blocks) as b:
                residual(b)
            residual(blocks)
            dve.wait_ge(squares_made, blocks + 1)
            V.tensor_scalar(var_eps[:, :, :], squares[:, :, :], 1.0 / feats, EPS, ALU.mult, ALU.add).then_inc(eps_added, 1)
            dve.wait_ge(rstd_made, 1)
            V.tensor_tensor(shift[:, :, :], neg_mean[:, :, :], rstd[:, :, :], ALU.mult).then_inc(shift_made, 1)

        @block.tensor
        def _(pe):
            T = nc.tensor
            pe.wait_ge(w_in, 16 * 7)
            T.matmul(hid_ps[:, 0:1], w1u[:, :], u_col[:, :], start=True, stop=True).then_inc(u_done, 1)
            pe.wait_ge(ones_made, 1)
            T.matmul(y_ps[:, 0, 0:feats], ones[0:1, :], b2_row[:, :], start=True, stop=True).then_inc(b2_spread, 1)
            pe.wait_ge(x_in, 32)
            pe.wait_ge(ident_made, 1)
            pe.wait_ge(bias_made, 1)

            def turn_x(b):
                n = P if not isinstance(b, int) else block_parts(b)
                wait_some(pe, x_copied, b)
                for r in range(2):
                    last = T.transpose(hid_ps[:, r * n:(r + 1) * n], x_sb[0:n, b, r * feats:(r + 1) * feats], ident[0:n, 0:n])
                last.then_inc(x_turned, 1)
            for b in range(blocks + 1):
                turn_x(b)
            pe.wait_ge(bad_counted, 1)
            T.matmul(t_ps[0][:, 0, 0:1], ones[0:steps, :], bad_count[:, :], start=True, stop=True).then_inc(bad_summed, 1)
            pe.wait_ge(local_made, 1)
            for q in range(WINS * RUN // 4):
                if q >= 2:
                    pe.wait_ge(ids_copied, q - 1)
                for c in range(4):
                    w, r = divmod(4 * q + c, RUN)
                    last = T.transpose(t_ps[q % 2][:, c, 0:steps], dst_real[:, w, r:WIN:RUN], ident[0:steps, 0:steps])
                last.then_inc(ids_turned, 1)
            pe.wait_ge(ids_copied, WINS * RUN // 4)
            for g in range(GROUPS):
                T.transpose(t_ps[0][:, g, 0:steps], row_src[:, g, :, :].rearrange("s t j -> s (t j)"), ident[0:steps, 0:steps])
                last = T.transpose(t_ps[1][0:1, g, 0:steps], group_low[:, g:g + 1], ident[0:steps, 0:steps])
            last.then_inc(bases_turned, 1)

            def level1(j, i, s, k, arrived):
                pe.wait_ge(*arrived)
                pe.wait_ge(hot_made, k * steps + (s + 1))
                if not (isinstance(s, int) and isinstance(k, int) and s < 2):
                    pe.wait_ge(rows_copied, k * steps + (s - 1))
                src = tail if j is None else slots[:, j]
                for g in range(GROUPS):
                    for e in range(RUN):
                        for t in range(TILES):
                            w = g * TILES + t
                            last = T.matmul(rows_ps[i][t * SPAN:(t + 1) * SPAN, g, 0:feats], hot[i][:, w * RUN + e, :],
                                            src[:, w, e * feats:(e + 1) * feats], start=(e == 0), stop=(e == RUN - 1),
                                            tile_position=(0, t * SPAN))
                last.then_inc(level1_done, 1)

            def level2(i, s, k):
                pe.wait_ge(rows_copied, k * steps + (s + 1))
                pe.wait_ge(row_hot_made, k * steps + (s + 1))
                if not (isinstance(s, int) and isinstance(k, int) and s < 2):
                    pe.wait_ge(added1, k * steps + (s - 1))
                for g in range(GROUPS):
                    last = T.matmul(cols_ps[i][:, g, 0:COLS], rows[i][:, g, :], row_hot[i][:, g, :], start=True, stop=True)
                last.then_inc(level2_done, 1)

            def sweep(k):
                def arrived(j, r):
                    return edges_in[j], 16 * (k * fills(j) + (r + 1))
                level1(0, 0, 0, k, arrived(0, 0))
                for j in range(1, SLOTS):
                    level1(j, j % 2, j, k, arrived(j, 0))
                    level2((j - 1) % 2, j - 1, k)
                with pe.Fori(1, rounds) as r:
                    for j in range(SLOTS):
                        level1(j, j % 2, r * SLOTS + j, k, arrived(j, r))
                        level2((j - 1) % 2, r * SLOTS + (j - 1), k)
                level1(0, (full - 1) % 2, full - 1, k, arrived(0, rounds))
                level2((full - 2) % 2, full - 2, k)
                level1(None, full % 2, full, k, (tail_in, tail_loads))
                level2((full - 1) % 2, full - 1, k)
                level2(full % 2, full, k)

            pe.wait_ge(x_copied, blocks + 1)
            sweep(0)
            more_sweeps(pe, sweep)

            def products(b):
                n = P if not isinstance(b, int) else block_parts(b)
                wait_some(pe, hid_made, b)
                T.matmul(hid_ps[:, 0:2 * n], w1x[:, :], x_t[:, bass.ds(b, 1), 0:2 * n].rearrange("f o n -> f (o n)"), start=True, stop=False)
                T.matmul(hid_ps[:, 0:2 * n], w1a[:, :], agg_t[:, bass.ds(b * pair, 2 * n)], start=False, stop=True).then_inc(hid_done, 1)
                pe.wait_ge(hid_made, b + 1)
                wait_some(pe, z_made, b)
                for r in range(2):
                    last = T.matmul(y_ps[0:n, r, 0:feats], hid[0][:, r:2 * n:2], w2_sb[:, :], start=True, stop=True)
                last.then_inc(y_done, 1)
            pe.wait_ge(added1, steps)
            products(0)
            with pe.Fori(1, blocks) as b:
                products(b)
            products(blocks)


_USED = ["x", "dst", "edge_attr_128", "L0_gnn_u", "L0_gnn_W1", "L0_gnn_b1", "L0_gnn_W2", "L0_gnn_b2"]


def kernel(**inputs):
    import numpy as np
    import concourse.bacc as bacc
    from concourse.bass_utils import run_bass_kernel_spmd

    nc = bacc.Bacc("TRN2", target_bir_lowering=False, num_devices=1)
    arrays, args = {}, []
    for name in _USED:
        a = np.ascontiguousarray(inputs[name])
        arrays[f"in_{name}"] = a
        args.append(nc.dram_tensor(f"in_{name}", a.shape, mybir.dt.from_np(a.dtype), kind="ExternalInput").ap())
    shape = np.asarray(inputs["x"]).shape
    args.append(nc.dram_tensor("out_0", shape, F32, kind="ExternalOutput").ap())
    residual_gnn_layer(nc, *args)
    done = run_bass_kernel_spmd(nc, [arrays], core_ids=[0])
    return done.results[0]["out_0"]
```

```python
import concourse.bass as bass
from concourse import mybir
from contextlib import ExitStack

F32 = mybir.dt.float32
I32 = mybir.dt.int32
ALU = mybir.AluOpType
ACT = mybir.ActivationFunctionType
AX = mybir.AxisListType

P = 128
EPS = 1e-5
RUN = 2
WIN = RUN * P
SPAN = 32
TILES = P // SPAN
COLS = 96
GROUPS = 2
WINS = GROUPS * TILES
STEP = WINS * WIN
SLOTS = 8
TURNS = SLOTS // 2
HOTS = 4
CATCH = 2


def residual_gnn_layer(nc, x, dst, edge_attr, u, w1, b1, w2, b2, out):
    nodes, feats = x.shape
    edges = edge_attr.shape[0]
    ufeats = u.shape[1]
    full = edges // STEP
    steps = full + 1
    rest = edges - full * STEP
    rest_wins = rest // WIN
    rest_parts = (rest - rest_wins * WIN) // RUN
    rounds = full // SLOTS
    sweeps = -(-nodes // SPAN)
    pair = 2 * P
    shift = pair.bit_length() - 1
    blocks = nodes // pair
    last_parts = (nodes - blocks * pair) // 2
    turns = rounds * TURNS
    mask = (1 << blocks.bit_length()) - 1
    width = nodes + COLS + SPAN
    assert feats == P and steps <= P and rest % RUN == 0 and edges >= WIN
    assert full == rounds * SLOTS + 1 and rounds > 1
    assert nodes == blocks * pair + 2 * last_parts and last_parts and blocks > CATCH
    assert rest_parts and rest_wins

    edge_full = edge_attr[0:full * STEP, :].rearrange("(s w p r) f -> s p w (r f)", w=WINS, p=P, r=RUN)
    edge_rest = edge_attr[full * STEP:full * STEP + rest_wins * WIN, :].rearrange("(w p r) f -> p w (r f)", p=P, r=RUN)
    edge_last = edge_attr[full * STEP + rest_wins * WIN:edges, :].rearrange("(p r) f -> p (r f)", r=RUN)
    x_full = x[0:blocks * pair, :].rearrange("(b p r) f -> p b (r f)", p=P, r=2)
    x_last = x[blocks * pair:nodes, :].rearrange("(p r) f -> p (r f)", r=2)
    out_full = out[0:blocks * pair, :].rearrange("(b p r) f -> p b (r f)", p=P, r=2)
    out_last = out[blocks * pair:nodes, :].rearrange("(p r) f -> p (r f)", r=2)

    ctx = ExitStack()
    with ctx:
        def sb(name, shape, dt=F32):
            return ctx.enter_context(nc.sbuf_tensor(name, shape, dt))

        def pb(name, shape):
            return ctx.enter_context(nc.psum_tensor(name, shape, F32))

        def sem(name):
            return ctx.enter_context(nc.semaphore(name))

        bases = sb("bases", [1, steps + 2, GROUPS], I32)
        plan = sb("plan", [1, turns + TURNS], I32)
        flag = sb("flag", [1, 4], I32)
        slots = sb("slots", [P, SLOTS, WINS, RUN * feats])
        tail = sb("tail", [P, WINS, RUN * feats])
        dst_int = sb("dst_int", [steps, WINS, WIN], I32)
        dst_local = sb("dst_local", [steps, WINS, WIN])
        low = sb("low", [steps, WINS])
        high = sb("high", [steps, WINS])
        group_low = sb("group_low", [steps, GROUPS])
        group_high = sb("group_high", [steps, GROUPS])
        bad = sb("bad", [steps, 4, WINS])
        bad_count = sb("bad_count", [steps, 1])
        good = sb("good", [P, 1])
        offset = sb("offset", [steps, WINS])
        row_src = sb("row_src", [steps, GROUPS, TILES, SPAN])
        low_after = sb("low_after", [1, steps])
        whole = sb("whole", [1, turns], I32)
        whole_f = sb("whole_f", [1, turns])
        begun = sb("begun", [1, turns])
        edge_node = sb("edge_node", [P, steps, WINS * RUN])
        row_node = sb("row_node", [P, steps, GROUPS])
        iota_int = sb("iota_int", [P, P], I32)
        iota = sb("iota", [P, P])
        iota_span = sb("iota_span", [P, SPAN])
        ident = sb("ident", [P, P])
        ones = sb("ones", [P, P])
        hot = [sb(f"hot{i}", [P, WINS * RUN, SPAN]) for i in range(HOTS)]
        row_hot = [sb(f"row_hot{i}", [P, GROUPS, COLS]) for i in range(HOTS)]
        rows = [sb(f"rows{i}", [P, GROUPS, feats]) for i in range(2)]
        agg_t = sb("agg_t", [P, width])
        x_sb = sb("x_sb", [P, blocks + 1, pair])
        z = sb("z", [P, blocks + 1, 2, feats])
        x_stage = sb("x_stage", [P, pair])
        x_t = sb("x_t", [P, pair])
        hid = sb("hid", [P, pair])
        w1x = sb("w1x", [P, feats])
        w1a = sb("w1a", [P, feats])
        w1u = sb("w1u", [ufeats, feats])
        w2_sb = sb("w2_sb", [P, feats])
        u_col = sb("u_col", [ufeats, 1])
        b1_col = sb("b1_col", [P, 1])
        bias = sb("bias", [P, 1])
        b2_row = sb("b2_row", [1, feats])
        b2_all = sb("b2_all", [P, feats])
        total = sb("total", [P, blocks + 1, 2])
        neg_mean = sb("neg_mean", [P, blocks + 1, 2])
        squares = sb("squares", [P, blocks + 1, 2])
        scratch = sb("scratch", [P, 2, feats])
        var_eps = sb("var_eps", [P, blocks + 1, 2])
        var = sb("var", [P, blocks + 1, 2])
        one_in_feats = sb("one_in_feats", [P, 2])
        eps = sb("eps", [P, 2])
        minus_half = sb("minus_half", [P, 2])
        rstd = sb("rstd", [P, blocks + 1, 2])

        rows_ps = [pb(f"rows_ps{i}", [P, GROUPS, 256]) for i in range(2)]
        cols_ps = [pb(f"cols_ps{i}", [P, GROUPS, 256]) for i in range(2)]
        t_ps = [pb(f"t_ps{i}", [P, 4, P]) for i in range(2)]
        x_ps = t_ps[0][:, 0:2, :].rearrange("p r n -> p (r n)")
        hid_ps = pb("hid_ps", [P, 512])
        y_ps = pb("y_ps", [P, 2, 256])

        edges_in = [sem(f"edges_in{j}") for j in range(SLOTS)]
        tail_zero = sem("tail_zero")
        tail_in = sem("tail_in")
        dst_in = sem("dst_in")
        x_in = sem("x_in")
        w_in = sem("w_in")
        iota_made = sem("iota_made")
        ident_made = sem("ident_made")
        ones_made = sem("ones_made")
        agg_zero = sem("agg_zero")
        prep = sem("prep")
        bad_counted = sem("bad_counted")
        bad_summed = sem("bad_summed")
        flag_made = sem("flag_made")
        local_made = sem("local_made")
        ids_turned = sem("ids_turned")
        ids_copied = sem("ids_copied")
        bases_turned = sem("bases_turned")
        bases_made = sem("bases_made")
        plan_made = sem("plan_made")
        consts_made = sem("consts_made")
        hot_made = sem("hot_made")
        row_hot_made = sem("row_hot_made")
        level1_done = sem("level1_done")
        rows_copied = sem("rows_copied")
        level2_done = sem("level2_done")
        added0 = sem("added0")
        added1 = sem("added1")
        z_ready = sem("z_ready")
        x_staged = sem("x_staged")
        x_turned = sem("x_turned")
        x_copied = sem("x_copied")
        hid_done = sem("hid_done")
        hid_made = sem("hid_made")
        y_done = sem("y_done")
        z_made = sem("z_made")
        mean_made = sem("mean_made")
        squares_made = sem("squares_made")
        var_made = sem("var_made")
        eps_added = sem("eps_added")
        rstd_made = sem("rstd_made")
        normed = sem("normed")
        out_stored = sem("out_stored")

        block = ctx.enter_context(nc.Block())

        def parts(b):
            return last_parts if isinstance(b, int) and b == blocks else P

        def ints(eng, row, least, most):
            return nc.values_load_multi_w_load_instructions(
                row, engines=[eng.engine], min_val=least, max_val=most, skip_runtime_bounds_check_because="the vector engine keeps them in these bounds")[1]

        def more_sweeps(eng, sweep):
            eng.wait_ge(flag_made, 1)
            enough = eng.value_load(flag[0:1, 0:1], min_val=0, max_val=1)
            with eng.If(enough < 1):
                with eng.Fori(1, sweeps) as k:
                    sweep(k)
                eng.wait_ge(added1, sweeps * steps)

        class Turns:

            def __init__(self, eng, r):
                self.eng = eng
                n = TURNS if isinstance(r, int) else 2 * TURNS
                at = r * TURNS
                self.begun = ints(eng, plan[0:1, bass.ds(at, n)], 0, blocks - CATCH)

            def stage(self, turn, what):
                at, after = self.begun[turn - 1], self.begun[turn]
                with self.eng.If(at < after):
                    what(self.eng.snap(at & mask, min_val=0, max_val=blocks - CATCH - 1))

        def late_blocks(eng, in_order, catch_up):
            begun_all = eng.value_load(plan[0:1, turns + TURNS - 1:turns + TURNS], min_val=0, max_val=blocks - CATCH)
            with eng.If(begun_all < blocks - CATCH):
                with eng.Fori(0, blocks - CATCH) as b:
                    with eng.If(begun_all < b + 1):
                        in_order(b)
            catch_up(range(blocks - CATCH, blocks + 1))

        def fills(j):
            return rounds + (1 if j == 0 else 0)

        pads = [(rest, WIN - rest % WIN)] + [(w * WIN, WIN) for w in range(rest_wins + 1, WINS)]
        dst_loads = 16 * (2 + len(pads))

        @block.sync
        def _(sp):
            def load(j, s):
                sp.dma_start(slots[:, j, :, :], edge_full[s]).then_inc(edges_in[j], 16)

            def refill(k):
                with sp.Fori(0, rounds - 1) as r:
                    for j in range(SLOTS):
                        sp.wait_ge(level1_done, r * SLOTS + (j + 1) + k * steps)
                        load(j, (r + 1) * SLOTS + j)
                sp.wait_ge(level1_done, k * steps + (full - SLOTS))
                load(0, full - 1)

            def sweep(k):
                sp.wait_ge(level1_done, k * steps)
                for j in range(SLOTS):
                    load(j, j)
                refill(k)

            sp.dma_start(dst_int[0:full, :, :], dst[0:full * STEP].rearrange("(s w e) -> s w e", w=WINS, e=WIN)).then_inc(dst_in, 16)
            last_row = dst_int[full:steps, :, :].rearrange("s w e -> s (w e)")
            sp.dma_start(last_row[:, 0:rest], dst[full * STEP:edges].rearrange("(s e) -> s e", s=1)).then_inc(dst_in, 16)
            for at, n in pads:
                sp.dma_start(last_row[:, at:at + n], dst[edges - n:edges].rearrange("(s e) -> s e", s=1)).then_inc(dst_in, 16)
            for j in range(SLOTS):
                load(j, j)
            sp.dma_start(x_sb[:, 0:blocks, :], x_full).then_inc(x_in, 16)
            sp.dma_start(x_sb[0:last_parts, blocks, :], x_last).then_inc(x_in, 16)
            sp.wait_ge(tail_zero, 1)
            sp.dma_start(tail[:, 0:rest_wins, :], edge_rest).then_inc(tail_in, 16)
            sp.dma_start(tail[0:rest_parts, rest_wins, :], edge_last).then_inc(tail_in, 16)
            refill(0)
            more_sweeps(sp, sweep)

        @block.gpsimd
        def _(pool):
            G = nc.gpsimd
            G.iota(iota_int[:, :], [[1, P]], base=0, channel_multiplier=0).then_inc(iota_made, 1)
            G.memset(ones[:, :], 1.0).then_inc(ones_made, 1)
            pool.wait_ge(ones_made, 1)
            G.affine_select(out=ident[:, :], in_=ones[:, :], compare_op=ALU.is_equal, fill=0.0,
                            base=0, pattern=[[-1, P]], channel_multiplier=1).then_inc(ident_made, 1)
            G.memset(agg_t[:, :], 0.0).then_inc(agg_zero, 1)
            G.memset(tail[:, :, :], 0.0).then_inc(tail_zero, 1)
            G.memset(one_in_feats[:, :], 1.0 / feats)
            G.memset(eps[:, :], EPS)
            G.memset(minus_half[:, :], -0.5).then_inc(consts_made, 1)
            G.memset(scratch[:, :, :], 0.0).then_inc(squares_made, 1)
            pool.wait_ge(x_in, 32)
            pool.wait_ge(z_made, 1)
            G.tensor_tensor(z[:, 0:blocks, :, :].rearrange("p b r f -> p (b r) f"),
                            x_sb[:, 0:blocks, :].rearrange("p b (r f) -> p (b r) f", r=2),
                            b2_all[:, :].unsqueeze(1).broadcast_to([P, 2 * blocks, feats]), ALU.add)
            n = last_parts
            G.tensor_tensor(z[0:n, blocks, :, :], x_sb[0:n, blocks, :].rearrange("p (r f) -> p r f", r=2),
                            b2_all[0:n, :].unsqueeze(1).broadcast_to([n, 2, feats]), ALU.add).then_inc(z_ready, 1)

            def reciprocal_deviation(b):
                n = parts(b)
                pool.wait_ge(squares_made, b + 2)
                G.tensor_tensor(var[0:n, bass.ds(b, 1), :], squares[0:n, bass.ds(b, 1), :],
                                one_in_feats[0:n, :].unsqueeze(1), ALU.mult).then_inc(var_made, 1)
                pool.wait_ge(var_made, b + 1)
                G.tensor_tensor(var_eps[0:n, bass.ds(b, 1), :], var[0:n, bass.ds(b, 1), :],
                                eps[0:n, :].unsqueeze(1), ALU.add).then_inc(eps_added, 1)
                pool.wait_ge(eps_added, b + 1)
                G.tensor_tensor(rstd[0:n, bass.ds(b, 1), :], var_eps[0:n, bass.ds(b, 1), :],
                                minus_half[0:n, :].unsqueeze(1), ALU.pow).then_inc(rstd_made, 1)

            def store(b):
                pool.wait_ge(normed, b + 1)
                to = out_last if parts(b) < P else out_full[:, bass.ds(b, 1), :]
                fr = z[0:parts(b), blocks, :, :].rearrange("p r f -> p (r f)") if parts(b) < P \
                    else z[:, bass.ds(b, 1), :, :].rearrange("p o r f -> p o (r f)")
                pool.dma_start(to, fr).then_inc(out_stored, 16)

            pool.wait_ge(consts_made, 1)
            reciprocal_deviation(0)
            with pool.Fori(1, blocks) as b:
                reciprocal_deviation(b)
                store(b - 1)
            reciprocal_deviation(blocks)
            store(blocks - 1)
            store(blocks)
            pool.wait_ge(out_stored, 16 * (blocks + 1))

        @block.scalar
        def _(act):
            A = nc.scalar
            act.dma_start(w1x[:, :], w1[0:feats, :]).then_inc(w_in, 16)
            act.dma_start(w1a[:, :], w1[feats:2 * feats, :]).then_inc(w_in, 16)
            act.dma_start(w1u[:, :], w1[2 * feats:2 * feats + ufeats, :]).then_inc(w_in, 16)
            act.dma_start(w2_sb[:, :], w2).then_inc(w_in, 16)
            act.dma_start(u_col[:, :], u[0:1, :].rearrange("a c -> c a")).then_inc(w_in, 16)
            act.dma_start(b1_col[:, :], b1.rearrange("(c a) -> c a", a=1)).then_inc(w_in, 16)
            act.dma_start(b2_row[:, :], b2.rearrange("(a c) -> a c", a=1)).then_inc(w_in, 16)
            act.wait_ge(hid_done, 1)
            A.activation(bias[:, :], hid_ps[:, 0:1], ACT.Identity, bias=b1_col[:, :]).then_inc(hid_made, 1)
            act.wait_ge(y_done, 1)
            A.activation(b2_all[:, :], y_ps[:, 0, 0:feats], ACT.Copy).then_inc(z_made, 1)

            def copy_rows(i, s, k):
                act.wait_ge(level1_done, k * steps + (s + 1))
                if not (isinstance(s, int) and isinstance(k, int) and s < 2):
                    act.wait_ge(level2_done, k * steps + (s - 1))
                A.activation(rows[i][:, :, :], rows_ps[i][:, :, 0:feats], ACT.Copy).then_inc(rows_copied, 1)

            def stage_x(b):
                n = parts(b)
                act.wait_ge(x_turned, b + 1)
                A.activation(x_stage[0:n, :], x_sb[0:n, bass.ds(b, 1), :].rearrange("p o n -> p (o n)"), ACT.Copy).then_inc(x_staged, 1)

            def copy_x(b):
                n = parts(b)
                act.wait_ge(x_turned, b + 2)
                act.wait_ge(hid_done, b + 1)
                A.activation(x_t[:, 0:2 * n].rearrange("f (p r) -> f r p", r=2),
                             x_ps[:, 0:2 * n].rearrange("f (r p) -> f r p", r=2), ACT.Copy).then_inc(x_copied, 1)

            def relu(b):
                n = parts(b)
                act.wait_ge(hid_done, b + 2)
                act.wait_ge(y_done, b + 1)
                A.activation(hid[:, 0:2 * n], hid_ps[:, 0:2 * n], ACT.Relu, bias=bias[:, :]).then_inc(hid_made, 1)

            def square(b):
                n = parts(b)
                act.wait_ge(mean_made, b + 1)
                act.wait_ge(squares_made, b + 1)
                for r in range(2):
                    last = A.activation(scratch[0:n, r, :], z[0:n, bass.ds(b, 1), r, :].rearrange("p o f -> p (o f)"), ACT.Square,
                                        bias=neg_mean[0:n, bass.ds(b, 1), r], accum_out=squares[0:n, bass.ds(b, 1), r])
                last.then_inc(squares_made, 1)

            def sweep(k):
                for j in range(SLOTS):
                    copy_rows(j % 2, j, k)
                with act.Fori(1, rounds) as r:
                    for j in range(SLOTS):
                        copy_rows(j % 2, r * SLOTS + j, k)
                copy_rows((full - 1) % 2, full - 1, k)
                copy_rows(full % 2, full, k)

            for j in range(SLOTS):
                copy_rows(j % 2, j, 0)
            act.wait_ge(plan_made, 1)
            act.wait_ge(x_in, 32)
            act.wait_ge(hid_made, 1)
            with act.Fori(1, rounds) as r:
                turn = Turns(act, r)
                for j in range(SLOTS):
                    t = TURNS + j // 2
                    if j % 2 == 0:
                        turn.stage(t, stage_x)
                        copy_rows(j % 2, r * SLOTS + j, 0)
                        turn.stage(t - 2, square)
                        turn.stage(t, copy_x)
                    else:
                        copy_rows(j % 2, r * SLOTS + j, 0)
                        turn.stage(t, relu)
            last_turns = Turns(act, rounds)
            copy_rows((full - 1) % 2, full - 1, 0)
            last_turns.stage(TURNS - 2, square)
            copy_rows(full % 2, full, 0)
            last_turns.stage(TURNS - 1, square)
            more_sweeps(act, sweep)

            def in_order(b):
                stage_x(b)
                copy_x(b)
                relu(b)
                square(b)

            def catch_up(left):
                stage_x(left[0])
                copy_x(left[0])
                stage_x(left[1])
                for n, b in enumerate(left):
                    relu(b)
                    if n + 1 < len(left):
                        copy_x(left[n + 1])
                    if n + 2 < len(left):
                        stage_x(left[n + 2])
                    square(b)
            late_blocks(act, in_order, catch_up)

        @block.vector
        def _(dve):
            V = nc.vector
            count = [0]

            def then(ins):
                count[0] += 1
                ins.then_inc(prep, 1)
                dve.wait_ge(prep, count[0])

            dve.wait_ge(iota_made, 1)
            V.tensor_copy(iota[:, :], iota_int[:, :]).then_inc(iota_made, 1)
            V.tensor_copy(iota_span[:, :], iota_int[:, 0:SPAN]).then_inc(iota_made, 1)
            V.memset(bad[:, :, :], 0.0)
            V.memset(bases[:, :, :], 0)
            then(V.memset(plan[:, :], 0))
            dve.wait_ge(iota_made, 3)
            dve.wait_ge(dst_in, dst_loads)
            V.tensor_reduce(low[:, :], dst_int[:, :, :], AX.X, ALU.min)
            then(V.tensor_reduce(high[:, :], dst_int[:, :, :], AX.X, ALU.max))
            V.tensor_scalar(bad[:, 0, :], low[:, :], 0.0, None, ALU.is_lt)
            V.tensor_scalar(bad[:, 1, :], high[:, :], float(nodes), None, ALU.is_ge)
            V.scalar_tensor_tensor(bad[:, 2, :], low[:, :], float(SPAN), high[:, :], ALU.add, ALU.is_le)
            V.tensor_reduce(group_low[:, :], low[:, :].rearrange("s (g t) -> s g t", g=GROUPS), AX.X, ALU.min)
            then(V.tensor_reduce(group_high[:, :], high[:, :].rearrange("s (g t) -> s g t", g=GROUPS), AX.X, ALU.max))
            then(V.scalar_tensor_tensor(bad[:, 3, 0:GROUPS], group_low[:, :], float(COLS), group_high[:, :], ALU.add, ALU.is_le))
            V.tensor_reduce(bad_count[:, :], bad[:, :, :], AX.XY, ALU.add).then_inc(bad_counted, 1)
            dve.wait_ge(bad_summed, 1)
            then(V.tensor_scalar(good[:, :], t_ps[0][:, 0, 0:1], 0.0, None, ALU.is_equal))
            V.tensor_copy(flag[:, 0:1], good[0:1, :]).then_inc(flag_made, 1)
            V.tensor_scalar(low[:, :], low[:, :], good[0:steps, :], None, ALU.mult)
            then(V.tensor_scalar(group_low[:, :], group_low[:, :], good[0:steps, :], None, ALU.mult))
            V.tensor_tensor(offset[:, :].rearrange("s (g t) -> s g t", g=GROUPS), low[:, :].rearrange("s (g t) -> s g t", g=GROUPS),
                            group_low[:, :].unsqueeze(2).broadcast_to([steps, GROUPS, TILES]), ALU.subtract)
            then(V.tensor_tensor(dst_local[:, :, :], dst_int[:, :, :], low[:, :].unsqueeze(2).broadcast_to([steps, WINS, WIN]), ALU.subtract))
            V.tensor_tensor(row_src[:, :, :, :].rearrange("s g t j -> s (g t) j"),
                            offset[:, :].unsqueeze(2).broadcast_to([steps, WINS, SPAN]),
                            iota[0:steps, 0:SPAN].unsqueeze(1).broadcast_to([steps, WINS, SPAN]), ALU.add).then_inc(local_made, 1)
            for q in range(WINS * RUN // 4):
                dve.wait_ge(ids_turned, q + 1)
                V.tensor_copy(edge_node[:, :, 4 * q:4 * q + 4].rearrange("p s c -> p c s"), t_ps[q % 2][:, :, 0:steps]).then_inc(ids_copied, 1)
            dve.wait_ge(bases_turned, 1)
            V.tensor_copy(bases[:, 0:steps, :].rearrange("p s g -> p g s"), t_ps[1][0:1, 0:GROUPS, 0:steps]).then_inc(bases_made, 1)
            dve.wait_ge(x_turned, 1)
            V.tensor_copy(row_node[:, :, :].rearrange("p s g -> p g s"), t_ps[0][:, 0:GROUPS, 0:steps]).then_inc(x_copied, 1)
            dve.wait_ge(bases_made, 1)
            dve.wait_ge(agg_zero, 1)

            def make_hot(i, s, k):
                known = isinstance(s, int) and isinstance(k, int)
                if not (known and s < HOTS):
                    dve.wait_ge(level1_done, k * steps + (s - HOTS + 1))
                elif s == 0:
                    dve.wait_ge(ids_copied, WINS * RUN // 4)
                    dve.wait_ge(x_copied, 1)
                V.tensor_tensor(hot[i][:, :, :],
                                edge_node[:, bass.ds(s, 1), :].rearrange("p o c -> p (o c)").unsqueeze(2).broadcast_to([P, WINS * RUN, SPAN]),
                                iota_span[:, :].unsqueeze(1).broadcast_to([P, WINS * RUN, SPAN]), ALU.is_equal).then_inc(hot_made, 1)
                if not (known and s < HOTS):
                    dve.wait_ge(level2_done, k * steps + (s - HOTS + 1))
                V.tensor_tensor(row_hot[i][:, :, :],
                                row_node[:, bass.ds(s, 1), :].rearrange("p o g -> p (o g)").unsqueeze(2).broadcast_to([P, GROUPS, COLS]),
                                iota[:, 0:COLS].unsqueeze(1).broadcast_to([P, GROUPS, COLS]), ALU.is_equal).then_inc(row_hot_made, 1)

            def add_cols(i, s, k, at):
                dve.wait_ge(level2_done, k * steps + (s + 1))
                for g, (mine, other) in enumerate(((added0, added1), (added1, added0))):
                    cols = agg_t[:, bass.ds(at[g], COLS)]
                    if not (isinstance(s, int) and isinstance(k, int) and s == 0 and g == 0):
                        dve.wait_ge(other, k * steps + (s + g))
                    V.tensor_tensor(cols, cols, cols_ps[i][:, g, 0:COLS], ALU.add).then_inc(mine, 1)

            def group_bases(s, n):
                row = bases[:, bass.ds(s, n), :].rearrange("p s g -> p (s g)")
                return ints(dve, row, 0, nodes - 1)

            def residual(b):
                n = parts(b)
                dve.wait_ge(y_done, b + 2)
                for r in range(2):
                    zr = z[0:n, bass.ds(b, 1), r, :].rearrange("p o f -> p (o f)")
                    last = V.scalar_tensor_tensor(zr, y_ps[0:n, r, 0:feats], 1.0, zr, ALU.mult, ALU.add,
                                                  accum_out=total[0:n, bass.ds(b, 1), r])
                last.then_inc(z_made, 1)
                dve.wait_ge(z_made, b + 2)
                V.tensor_scalar(neg_mean[0:n, bass.ds(b, 1), :], total[0:n, bass.ds(b, 1), :], -1.0 / feats, None, ALU.mult).then_inc(mean_made, 1)

            def normalise(b):
                n = parts(b)
                dve.wait_ge(rstd_made, b + 1)
                for r in range(2):
                    zr = z[0:n, bass.ds(b, 1), r, :].rearrange("p o f -> p (o f)")
                    last = V.tensor_scalar(zr, zr, neg_mean[0:n, bass.ds(b, 1), r], rstd[0:n, bass.ds(b, 1), r], ALU.add, ALU.mult)
                last.then_inc(normed, 1)

            def sweep(k):
                dve.wait_ge(hot_made, k * steps)
                V.tensor_scalar(iota_span[:, :], iota_span[:, :], float(SPAN), None, ALU.add).then_inc(iota_made, 1)
                dve.wait_ge(iota_made, k + 3)
                at = [k * SPAN, k * SPAN]
                make_hot(0, 0, k)
                make_hot(1, 1, k)
                for j in range(SLOTS):
                    make_hot((j + 2) % HOTS, j + 2, k)
                    if j:
                        add_cols((j - 1) % 2, j - 1, k, at)
                with dve.Fori(1, rounds) as r:
                    for j in range(SLOTS):
                        make_hot((j + 2) % HOTS, r * SLOTS + (j + 2), k)
                        add_cols((j - 1) % 2, r * SLOTS + (j - 1), k, at)
                for s in range(full - 2, steps):
                    add_cols(s % 2, s, k, at)

            make_hot(0, 0, 0)
            make_hot(1, 1, 0)
            make_hot(2, 2, 0)
            make_hot(3, 3, 0)
            then(V.tensor_tensor_scan(low_after[:, :], bases[:, steps - 1::-1, 0][:, 0:steps], bases[:, steps - 1::-1, 1][:, 0:steps],
                                      float(nodes), ALU.min, ALU.min))
            then(V.tensor_copy(whole[:, TURNS:turns], low_after[:, ::-1][:, SLOTS:2 * turns:2]))
            then(V.tensor_scalar(whole[:, TURNS:turns], whole[:, TURNS:turns], shift, None, ALU.arith_shift_right))
            then(V.tensor_scalar(whole_f[:, TURNS:turns], whole[:, TURNS:turns], float(blocks - CATCH), None, ALU.min))
            then(V.tensor_tensor_scan(begun[:, TURNS:turns], ones[0:1, TURNS:turns], whole_f[:, TURNS:turns], 0.0, ALU.add, ALU.min))
            V.tensor_copy(plan[:, 2 * TURNS:turns + TURNS], begun[:, TURNS:turns]).then_inc(plan_made, 1)

            at = group_bases(0, SLOTS)
            for j in range(SLOTS):
                if j + 2 >= HOTS:
                    make_hot((j + 2) % HOTS, j + 2, 0)
                if j:
                    add_cols((j - 1) % 2, j - 1, 0, at[2 * j - 2:])
            dve.wait_ge(plan_made, 1)
            dve.wait_ge(z_ready, 1)
            with dve.Fori(1, rounds) as r:
                at = group_bases(r * SLOTS - 1, SLOTS)
                turn = Turns(dve, r)
                for j in range(SLOTS):
                    t = TURNS + j // 2
                    make_hot((j + 2) % HOTS, r * SLOTS + (j + 2), 0)
                    add_cols((j - 1) % 2, r * SLOTS + (j - 1), 0, at[2 * j:])
                    if j % 2:
                        turn.stage(t - 1, residual)
                        turn.stage(t - 3, normalise)
            at = group_bases(full - 2, 3)
            last_turns = Turns(dve, rounds)
            add_cols((full - 2) % 2, full - 2, 0, at[0:])
            last_turns.stage(TURNS - 1, residual)
            last_turns.stage(TURNS - 3, normalise)
            add_cols((full - 1) % 2, full - 1, 0, at[2:])
            add_cols(full % 2, full, 0, at[4:])
            last_turns.stage(TURNS - 2, normalise)
            last_turns.stage(TURNS - 1, normalise)
            more_sweeps(dve, sweep)

            def in_order(b):
                residual(b)
                normalise(b)

            def catch_up(left):
                for n, b in enumerate(left):
                    residual(b)
                    if n:
                        normalise(left[n - 1])
                normalise(left[-1])
            late_blocks(dve, in_order, catch_up)

        @block.tensor
        def _(pe):
            T = nc.tensor
            pe.wait_ge(w_in, 16 * 7)
            T.matmul(hid_ps[:, 0:1], w1u[:, :], u_col[:, :], start=True, stop=True).then_inc(hid_done, 1)
            pe.wait_ge(ones_made, 1)
            T.matmul(y_ps[:, 0, 0:feats], ones[0:1, :], b2_row[:, :], start=True, stop=True).then_inc(y_done, 1)
            pe.wait_ge(ident_made, 1)
            pe.wait_ge(bad_counted, 1)
            T.matmul(t_ps[0][:, 0, 0:1], ones[0:steps, :], bad_count[:, :], start=True, stop=True).then_inc(bad_summed, 1)
            pe.wait_ge(local_made, 1)
            for q in range(WINS * RUN // 4):
                if q >= 2:
                    pe.wait_ge(ids_copied, q - 1)
                for c in range(4):
                    w, r = divmod(4 * q + c, RUN)
                    last = T.transpose(t_ps[q % 2][:, c, 0:steps], dst_local[:, w, r:WIN:RUN], ident[0:steps, 0:steps])
                last.then_inc(ids_turned, 1)
            pe.wait_ge(ids_copied, WINS * RUN // 4)
            for g in range(GROUPS):
                last = T.transpose(t_ps[1][0:1, g, 0:steps], group_low[:, g:g + 1], ident[0:steps, 0:steps])
            last.then_inc(bases_turned, 1)
            for g in range(GROUPS):
                last = T.transpose(t_ps[0][:, g, 0:steps], row_src[:, g, :, :].rearrange("s t j -> s (t j)"), ident[0:steps, 0:steps])
            last.then_inc(x_turned, 1)

            def level1(j, i, s, k, arrived):
                pe.wait_ge(*arrived)
                pe.wait_ge(hot_made, k * steps + (s + 1))
                if not (isinstance(s, int) and isinstance(k, int) and s < 2):
                    pe.wait_ge(rows_copied, k * steps + (s - 1))
                src = tail if j is None else slots[:, j]
                hot_s = hot[i % HOTS]
                for g in range(GROUPS):
                    for e in range(RUN):
                        for t in range(TILES):
                            w = g * TILES + t
                            last = T.matmul(rows_ps[i % 2][t * SPAN:(t + 1) * SPAN, g, 0:feats], hot_s[:, w * RUN + e, :],
                                            src[:, w, e * feats:(e + 1) * feats], start=(e == 0), stop=(e == RUN - 1),
                                            tile_position=(0, t * SPAN))
                last.then_inc(level1_done, 1)

            def level2(i, s, k):
                pe.wait_ge(rows_copied, k * steps + (s + 1))
                pe.wait_ge(row_hot_made, k * steps + (s + 1))
                if not (isinstance(s, int) and isinstance(k, int) and s < 2):
                    pe.wait_ge(added1, k * steps + (s - 1))
                for g in range(GROUPS):
                    last = T.matmul(cols_ps[i % 2][:, g, 0:COLS], rows[i % 2][:, g, :], row_hot[i % HOTS][:, g, :], start=True, stop=True)
                last.then_inc(level2_done, 1)

            def turn_x(b):
                n = parts(b)
                pe.wait_ge(x_staged, b + 1)
                pe.wait_ge(x_copied, b + 1)
                for r in range(2):
                    last = T.transpose(x_ps[:, r * n:(r + 1) * n], x_stage[0:n, r * feats:(r + 1) * feats], ident[0:n, 0:n])
                last.then_inc(x_turned, 1)

            def product1(b):
                n = parts(b)
                pe.wait_ge(x_copied, b + 2)
                pe.wait_ge(hid_made, b + 1)
                T.matmul(hid_ps[:, 0:2 * n], w1x[:, :], x_t[:, 0:2 * n], start=True, stop=False)
                T.matmul(hid_ps[:, 0:2 * n], w1a[:, :], agg_t[:, bass.ds(b * pair, 2 * n)], start=False, stop=True).then_inc(hid_done, 1)

            def product2(b):
                n = parts(b)
                pe.wait_ge(hid_made, b + 2)
                pe.wait_ge(z_made, b + 1)
                for r in range(2):
                    last = T.matmul(y_ps[0:n, r, 0:feats], hid[:, r:2 * n:2], w2_sb[:, :], start=True, stop=True)
                last.then_inc(y_done, 1)

            def arrived(j, r, k):
                return edges_in[j], 16 * (k * fills(j) + (r + 1))

            def sweep(k):
                level1(0, 0, 0, k, arrived(0, 0, k))
                for j in range(1, SLOTS):
                    level1(j, j, j, k, arrived(j, 0, k))
                    level2(j - 1, j - 1, k)
                with pe.Fori(1, rounds) as r:
                    for j in range(SLOTS):
                        level1(j, j, r * SLOTS + j, k, arrived(j, r, k))
                        level2(j - 1, r * SLOTS + (j - 1), k)
                last_steps(k)

            def last_steps(k):
                level1(0, full - 1, full - 1, k, arrived(0, rounds, k))
                level2(full - 2, full - 2, k)
                level1(None, full, full, k, (tail_in, 32))
                level2(full - 1, full - 1, k)
                level2(full, full, k)

            level1(0, 0, 0, 0, arrived(0, 0, 0))
            for j in range(1, SLOTS):
                level1(j, j, j, 0, arrived(j, 0, 0))
                level2(j - 1, j - 1, 0)
            pe.wait_ge(plan_made, 1)
            with pe.Fori(1, rounds) as r:
                turn = Turns(pe, r)
                for j in range(SLOTS):
                    t = TURNS + j // 2
                    level1(j, j, r * SLOTS + j, 0, arrived(j, r, 0))
                    level2(j - 1, r * SLOTS + (j - 1), 0)
                    if j % 2 == 0:
                        turn.stage(t, turn_x)
                        turn.stage(t - 1, product2)
                    else:
                        pe.wait_ge(added1, r * SLOTS + (j - 1))
                        turn.stage(t, product1)
            Turns(pe, rounds).stage(TURNS - 1, product2)
            last_steps(0)
            more_sweeps(pe, sweep)
            pe.wait_ge(added1, steps)

            def in_order(b):
                turn_x(b)
                product1(b)
                product2(b)

            def catch_up(left):
                turn_x(left[0])
                for n, b in enumerate(left):
                    product1(b)
                    if n + 1 < len(left):
                        turn_x(left[n + 1])
                    product2(b)
            late_blocks(pe, in_order, catch_up)


_USED = ["x", "dst", "edge_attr_128", "L0_gnn_u", "L0_gnn_W1", "L0_gnn_b1", "L0_gnn_W2", "L0_gnn_b2"]


def kernel(**inputs):
    import numpy as np
    import concourse.bacc as bacc
    from concourse.bass_utils import run_bass_kernel_spmd

    nc = bacc.Bacc("TRN2", target_bir_lowering=False, num_devices=1)
    arrays, args = {}, []
    for name in _USED:
        a = np.ascontiguousarray(inputs[name])
        arrays[f"in_{name}"] = a
        args.append(nc.dram_tensor(f"in_{name}", a.shape, mybir.dt.from_np(a.dtype), kind="ExternalInput").ap())
    shape = np.asarray(inputs["x"]).shape
    args.append(nc.dram_tensor("out_0", shape, F32, kind="ExternalOutput").ap())
    residual_gnn_layer(nc, *args)
    done = run_bass_kernel_spmd(nc, [arrays], core_ids=[0])
    return done.results[0]["out_0"]
```

```python
import concourse.bass as bass
from concourse import mybir
from contextlib import ExitStack

F32 = mybir.dt.float32
I32 = mybir.dt.int32
ALU = mybir.AluOpType
ACT = mybir.ActivationFunctionType
AX = mybir.AxisListType

P = 128
EPS = 1e-5
RUN = 2
WIN = RUN * P
SPAN = 32
TILES = P // SPAN
COLS = 96
GROUPS = 2
WINS = GROUPS * TILES
STEP = WINS * WIN
SLOTS = 8
TURNS = SLOTS // 2
HOTS = 4
LEAD = 4


def residual_gnn_layer(nc, x, dst, edge_attr, u, w1, b1, w2, b2, out):
    nodes, feats = x.shape
    edges = edge_attr.shape[0]
    ufeats = u.shape[1]
    full = edges // STEP
    steps = full + 1
    rest = edges - full * STEP
    rest_wins = rest // WIN
    rest_parts = (rest - rest_wins * WIN) // RUN
    rounds = full // SLOTS
    sweeps = -(-nodes // SPAN)
    pair = 2 * P
    shift = pair.bit_length() - 1
    blocks = nodes // pair
    last_parts = (nodes - blocks * pair) // 2
    turns = rounds * TURNS + 1
    mask = (1 << blocks.bit_length()) - 1
    width = max(nodes + COLS, (blocks + 1) * pair)
    assert feats == P and steps <= P and rest % RUN == 0 and edges >= WIN
    assert full == rounds * SLOTS + 1 and rounds > 1
    assert nodes == blocks * pair + 2 * last_parts and last_parts and blocks % 2 == 0 and blocks > LEAD
    assert rest_parts and rest_wins > TILES and GROUPS == 2

    edge_full = edge_attr[0:full * STEP, :].rearrange("(s w p r) f -> s p w (r f)", w=WINS, p=P, r=RUN)
    edge_rest = edge_attr[full * STEP:full * STEP + rest_wins * WIN, :].rearrange("(w p r) f -> p w (r f)", p=P, r=RUN)
    edge_last = edge_attr[full * STEP + rest_wins * WIN:edges, :].rearrange("(p r) f -> p (r f)", r=RUN)
    x_full = x[0:blocks * pair, :].rearrange("(b p r) f -> p b (r f)", p=P, r=2)
    x_last = x[blocks * pair:nodes, :].rearrange("(p r) f -> p (r f)", r=2)
    out_full = out[0:blocks * pair, :].rearrange("(b p r) f -> p b (r f)", p=P, r=2)
    out_last = out[blocks * pair:nodes, :].rearrange("(p r) f -> p (r f)", r=2)

    ctx = ExitStack()
    with ctx:
        def sb(name, shape, dt=F32):
            return ctx.enter_context(nc.sbuf_tensor(name, shape, dt))

        def pb(name, shape):
            return ctx.enter_context(nc.psum_tensor(name, shape, F32))

        def sem(name):
            return ctx.enter_context(nc.semaphore(name))

        bases = sb("bases", [1, steps + 3, GROUPS], I32)
        plan = sb("plan", [1, turns + TURNS + 1], I32)
        slots = sb("slots", [P, SLOTS, WINS, RUN * feats])
        head = sb("head", [P, WINS, RUN * feats])
        tail = sb("tail", [P, WINS, RUN * feats])
        dst_int = sb("dst_int", [steps, WINS, WIN], I32)
        dst_local = sb("dst_local", [steps, WINS, WIN])
        low = sb("low", [steps, WINS])
        high = sb("high", [steps, WINS])
        group_low = sb("group_low", [steps, GROUPS])
        group_high = sb("group_high", [steps, GROUPS])
        bad = sb("bad", [steps, 4, WINS])
        bad_count = sb("bad_count", [steps, 1])
        good = sb("good", [P, 1])
        offset = sb("offset", [steps, WINS])
        row_src = sb("row_src", [steps, GROUPS, TILES, SPAN])
        low_after = sb("low_after", [1, steps])
        whole = sb("whole", [1, turns], I32)
        whole_f = sb("whole_f", [1, turns])
        begun = sb("begun", [1, turns])
        edge_node = sb("edge_node", [P, steps, WINS * RUN])
        row_node = sb("row_node", [P, steps, GROUPS])
        iota_int = sb("iota_int", [P, P], I32)
        iota = sb("iota", [P, P])
        iota_span = sb("iota_span", [P, SPAN])
        ident = sb("ident", [P, P])
        ones = sb("ones", [P, P])
        hot = [sb(f"hot{i}", [P, WINS * RUN, SPAN]) for i in range(HOTS)]
        row_hot = [sb(f"row_hot{i}", [P, GROUPS, COLS]) for i in range(HOTS)]
        rows = [sb(f"rows{i}", [P, GROUPS, feats]) for i in range(2)]
        agg_t = sb("agg_t", [P, width])
        z = sb("z", [P, blocks + 1, 2, feats])
        x_t = sb("x_t", [P, blocks + 1, pair])
        hid = [sb(f"hid{i}", [P, pair]) for i in range(2)]
        w1x = sb("w1x", [P, feats])
        w1a = sb("w1a", [P, feats])
        w1u = sb("w1u", [ufeats, feats])
        w2_sb = sb("w2_sb", [P, feats])
        u_col = sb("u_col", [ufeats, 1])
        b1_col = sb("b1_col", [P, 1])
        bias = sb("bias", [P, 1])
        b2_row = sb("b2_row", [1, feats])
        b2_all = sb("b2_all", [P, feats])
        total = sb("total", [P, blocks + 1, 2])
        neg_mean = sb("neg_mean", [P, blocks + 1, 2])
        neg_scaled = sb("neg_scaled", [P, blocks + 1, 2])
        var = sb("var", [P, blocks + 1, 2])
        scratch = sb("scratch", [P, 2, feats])
        var_eps = sb("var_eps", [P, blocks + 1, 2])
        eps = sb("eps", [P, 2])
        minus_half = sb("minus_half", [P, 2])
        minus_share = sb("minus_share", [P, 2])
        rstd = sb("rstd", [P, blocks + 1, 2])

        rows_ps = [pb(f"rows_ps{i}", [P, GROUPS, 256]) for i in range(2)]
        cols_ps = [pb(f"cols_ps{i}", [P, GROUPS, 256]) for i in range(2)]
        t_ps = [pb(f"t_ps{i}", [P, 4, P]) for i in range(2)]
        hid_ps = pb("hid_ps", [P, 512])
        y_ps = pb("y_ps", [P, 2, 256])
        hid_bank = t_ps[0][:, :, :].rearrange("p c n -> p (c n)")
        y_bank = t_ps[1]

        edges_in = [sem(f"edges_in{j}") for j in range(SLOTS)]
        tail_zero = sem("tail_zero")
        head_in = sem("head_in")
        tail_in = [sem(f"tail_in{g}") for g in range(GROUPS)]
        dst_in = sem("dst_in")
        x_in = sem("x_in")
        w_in = sem("w_in")
        iota_made = sem("iota_made")
        ident_made = sem("ident_made")
        ones_made = sem("ones_made")
        agg_zero = sem("agg_zero")
        prep = sem("prep")
        bad_counted = sem("bad_counted")
        bad_summed = sem("bad_summed")
        local_made = sem("local_made")
        ids_turned = sem("ids_turned")
        ids_copied = sem("ids_copied")
        bases_turned = sem("bases_turned")
        rows_turned = sem("rows_turned")
        row_node_made = sem("row_node_made")
        bases_made = sem("bases_made")
        plan_made = sem("plan_made")
        consts_made = sem("consts_made")
        hot_made = sem("hot_made")
        row_hot_made = sem("row_hot_made")
        level1_done = sem("level1_done")
        rows_copied = sem("rows_copied")
        level2_done = sem("level2_done")
        tail_level1_done = sem("tail_level1_done")
        tail_rows_copied = sem("tail_rows_copied")
        tail_level2_done = sem("tail_level2_done")
        added0 = sem("added0")
        added1 = sem("added1")
        z_ready = sem("z_ready")
        x_turned = sem("x_turned")
        x_copied = sem("x_copied")
        hid_done = sem("hid_done")
        hid_made = sem("hid_made")
        y_done = sem("y_done")
        z_made = sem("z_made")
        mean_made = sem("mean_made")
        neg_made = sem("neg_made")
        var_made = sem("var_made")
        eps_added = sem("eps_added")
        rstd_made = sem("rstd_made")
        normed = sem("normed")
        out_stored = sem("out_stored")

        block = ctx.enter_context(nc.Block())

        def parts(b):
            return last_parts if isinstance(b, int) and b == blocks else P

        def ints(eng, row, least, most):
            return nc.values_load_multi_w_load_instructions(
                row, engines=[eng.engine], min_val=least, max_val=most, skip_runtime_bounds_check_because="the vector engine keeps them in these bounds")[1]

        def more_sweeps(eng, enough, sweep):
            with eng.If(enough < 1):
                with eng.Fori(1, sweeps) as k:
                    sweep(k)
                eng.wait_ge(added1, sweeps * steps)

        class Turns:

            def __init__(self, eng, r):
                self.eng = eng
                at = r * TURNS
                if isinstance(r, int):
                    self.begun = ints(eng, plan[0:1, at:], 0, blocks)
                    self.enough = self.begun[TURNS + 1]
                else:
                    self.begun = ints(eng, plan[0:1, bass.ds(at, 2 * TURNS)], 0, blocks)

            def stage(self, turn, what):
                at, after = self.begun[turn - 1], self.begun[turn]
                with self.eng.If(at < after):
                    what(self.eng.snap(at & mask, min_val=0, max_val=blocks - 1))

        def late_blocks(eng, last_turns, sweep, in_order):
            begun_all = last_turns.begun[TURNS]
            with eng.If(begun_all < blocks):
                more_sweeps(eng, last_turns.enough, sweep)
                with eng.Fori(0, blocks) as b:
                    with eng.If(begun_all < b + 1):
                        in_order(b)

        def ending(eng, last_turns, brief, general):
            at, after = last_turns.begun[0], last_turns.begun[TURNS]
            is_brief = eng.snap(after * 2 - at, min_val=0, max_val=2 * blocks)
            with eng.If(is_brief > blocks + TURNS - 1):
                brief()
            with eng.If(is_brief < blocks + TURNS):
                general()

        pads = [(rest, WIN - rest % WIN)] + [(w * WIN, WIN) for w in range(rest_wins + 1, WINS)]
        dst_loads = 16 * (2 + len(pads))

        x_turns = [range(2 * j, min(2 * j + 2, blocks // 2 + 1)) for j in range(SLOTS)]
        assert 2 * SLOTS > blocks // 2

        @block.sync
        def _(sp):
            def load(j, s):
                sp.dma_start(slots[:, j, :, :], edge_full[s]).then_inc(edges_in[j], 16)

            def refill(k):
                with sp.Fori(0, rounds - 1) as r:
                    for j in range(SLOTS):
                        sp.wait_ge(level1_done, r * SLOTS + (j + 2) + k * steps)
                        load(j, (r + 1) * SLOTS + (j + 1))

            def sweep(k):
                sp.wait_ge(level1_done, k * steps)
                for j in range(SLOTS):
                    load(j, j + 1)
                refill(k)

            def load_x(a, b):
                sp.dma_start(z[:, a:b, :, :].rearrange("p b r f -> p b (r f)"), x_full[:, a:b, :]).then_inc(x_in, 16)

            sp.dma_start(dst_int[0:full, :, :], dst[0:full * STEP].rearrange("(s w e) -> s w e", w=WINS, e=WIN)).then_inc(dst_in, 16)
            load_x(0, LEAD)
            last_row = dst_int[full:steps, :, :].rearrange("s w e -> s (w e)")
            sp.dma_start(last_row[:, 0:rest], dst[full * STEP:edges].rearrange("(s e) -> s e", s=1)).then_inc(dst_in, 16)
            for at, n in pads:
                sp.dma_start(last_row[:, at:at + n], dst[edges - n:edges].rearrange("(s e) -> s e", s=1)).then_inc(dst_in, 16)
            load_x(LEAD, blocks)
            sp.dma_start(z[0:last_parts, blocks, :, :].rearrange("p r f -> p (r f)"), x_last).then_inc(x_in, 16)
            sp.dma_start(w1x[:, :], w1[0:feats, :]).then_inc(w_in, 16)
            sp.dma_start(w1a[:, :], w1[feats:2 * feats, :]).then_inc(w_in, 16)
            sp.dma_start(w1u[:, :], w1[2 * feats:2 * feats + ufeats, :]).then_inc(w_in, 16)
            sp.dma_start(w2_sb[:, :], w2).then_inc(w_in, 16)
            sp.dma_start(u_col[:, :], u[0:1, :].rearrange("a c -> c a")).then_inc(w_in, 16)
            sp.dma_start(b1_col[:, :], b1.rearrange("(c a) -> c a", a=1)).then_inc(w_in, 16)
            sp.dma_start(b2_row[:, :], b2.rearrange("(a c) -> a c", a=1)).then_inc(w_in, 16)
            sp.dma_start(head[:, :, :], edge_full[0]).then_inc(head_in, 16)
            for j in range(SLOTS):
                load(j, j + 1)
            refill(0)
            sp.wait_ge(tail_zero, 1)
            sp.dma_start(tail[:, 0:TILES, :], edge_rest[:, 0:TILES, :]).then_inc(tail_in[0], 16)
            sp.dma_start(tail[:, TILES:rest_wins, :], edge_rest[:, TILES:rest_wins, :]).then_inc(tail_in[1], 16)
            sp.dma_start(tail[0:rest_parts, rest_wins, :], edge_last).then_inc(tail_in[1], 16)
            sp.wait_ge(plan_made, 1)
            more_sweeps(sp, sp.value_load(plan[0:1, turns + TURNS:turns + TURNS + 1], min_val=0, max_val=1), sweep)
            bounds = sorted({0, blocks // 3, 2 * blocks // 3, blocks - 4, blocks - 2, blocks - 1, blocks})
            for a, b in zip(bounds, bounds[1:]):
                sp.wait_ge(normed, b)
                sp.dma_start(out_full[:, a:b, :], z[:, a:b, :, :].rearrange("p b r f -> p b (r f)")).then_inc(out_stored, 16)
            sp.wait_ge(normed, blocks + 1)
            sp.dma_start(out_last, z[0:last_parts, blocks, :, :].rearrange("p r f -> p (r f)")).then_inc(out_stored, 16)
            sp.wait_ge(out_stored, 16 * len(bounds))

        @block.gpsimd
        def _(pool):
            G = nc.gpsimd
            G.iota(iota_int[:, :], [[1, P]], base=0, channel_multiplier=0).then_inc(iota_made, 1)
            G.memset(ones[:, :], 1.0).then_inc(ones_made, 1)
            pool.wait_ge(ones_made, 1)
            G.affine_select(out=ident[:, :], in_=ones[:, :], compare_op=ALU.is_equal, fill=0.0,
                            base=0, pattern=[[-1, P]], channel_multiplier=1).then_inc(ident_made, 1)
            G.memset(tail[:, rest_wins:WINS, :], 0.0).then_inc(tail_zero, 1)
            G.memset(agg_t[:, :], 0.0).then_inc(agg_zero, 1)
            G.memset(eps[:, :], EPS)
            G.memset(minus_share[:, :], -1.0 / feats)
            G.memset(minus_half[:, :], -0.5).then_inc(consts_made, 1)
            G.memset(scratch[:, :, :], 0.0).then_inc(var_made, 1)
            pool.wait_ge(z_made, 1)
            with pool.Fori(0, blocks // 2) as q:
                pool.wait_ge(x_turned, q + 1)
                two = z[:, bass.ds(q * 2, 2), :, :].rearrange("p b r f -> p (b r) f")
                G.tensor_tensor(two, two, b2_all[:, :].unsqueeze(1).broadcast_to([P, 4, feats]), ALU.add)
            n = last_parts
            pool.wait_ge(x_turned, blocks // 2 + 1)
            G.tensor_tensor(z[0:n, blocks, :, :], z[0:n, blocks, :, :],
                            b2_all[0:n, :].unsqueeze(1).broadcast_to([n, 2, feats]), ALU.add).then_inc(z_ready, 1)

            def reciprocal_deviation(b):
                n = parts(b)
                pool.wait_ge(z_made, b + 2)
                G.tensor_tensor(neg_mean[0:n, bass.ds(b, 1), :], total[0:n, bass.ds(b, 1), :],
                                minus_share[0:n, :].unsqueeze(1), ALU.mult).then_inc(neg_made, 1)
                pool.wait_ge(var_made, b + 2)
                G.tensor_tensor(var_eps[0:n, bass.ds(b, 1), :], var[0:n, bass.ds(b, 1), :],
                                eps[0:n, :].unsqueeze(1), ALU.add).then_inc(eps_added, 1)
                pool.wait_ge(eps_added, b + 1)
                G.tensor_tensor(rstd[0:n, bass.ds(b, 1), :], var_eps[0:n, bass.ds(b, 1), :],
                                minus_half[0:n, :].unsqueeze(1), ALU.pow).then_inc(rstd_made, 1)

            pool.wait_ge(consts_made, 1)
            with pool.Fori(0, blocks) as b:
                reciprocal_deviation(b)
            reciprocal_deviation(blocks)

        @block.scalar
        def _(act):
            A = nc.scalar
            act.wait_ge(hid_done, 1)
            A.activation(bias[:, :], hid_ps[:, 0:1], ACT.Identity, bias=b1_col[:, :]).then_inc(hid_made, 1)
            act.wait_ge(y_done, 1)
            A.activation(b2_all[:, :], y_ps[:, 0, 0:feats], ACT.Copy).then_inc(z_made, 1)

            turn_banks = [hid_ps[:, :], y_ps[:, :, :].rearrange("p r n -> p (r n)")]

            def copy_x(q):
                act.wait_ge(x_turned, q + 1)
                w, n = (1, last_parts) if q == blocks // 2 else (2, P)
                A.activation(x_t[:, bass.ds(q * 2, w), 0:2 * n].rearrange("f b (p r) -> f b r p", r=2),
                             turn_banks[q % 2][:, 0:w * 2 * n].rearrange("f (b r p) -> f b r p", b=w, r=2), ACT.Copy).then_inc(x_copied, 1)

            def copy_rows(s, k, i=None):
                i = (s if i is None else i) % 2
                act.wait_ge(level1_done, k * steps + (s + 1))
                if not (isinstance(s, int) and isinstance(k, int) and s < 2):
                    act.wait_ge(level2_done, k * steps + (s - 1))
                A.activation(rows[i][:, :, :], rows_ps[i][:, :, 0:feats], ACT.Copy).then_inc(rows_copied, 1)

            def copy_tail(k):
                i = full % 2
                act.wait_ge(tail_level1_done, k + 1)
                act.wait_ge(level2_done, k * steps + (full - 1))
                A.activation(rows[i][:, 0, :], rows_ps[i][:, 0, 0:feats], ACT.Copy).then_inc(tail_rows_copied, 1)
                act.wait_ge(level1_done, k * steps + steps)
                A.activation(rows[i][:, 1, :], rows_ps[1 - i][:, 1, 0:feats], ACT.Copy).then_inc(rows_copied, 1)

            def relu(b, n=0, bank=hid_ps):
                m = parts(b)
                act.wait_ge(hid_done, b + 2)
                if n == 0:
                    act.wait_ge(y_done, b + 1)
                A.activation(hid[n][:, 0:2 * m], bank[:, 0:2 * m], ACT.Relu, bias=bias[:, :]).then_inc(hid_made, 1)

            def square(b):
                n = parts(b)
                act.wait_ge(mean_made, b + 1)
                act.wait_ge(var_made, b + 1)
                for r in range(2):
                    last = A.activation(scratch[0:n, r, :], z[0:n, bass.ds(b, 1), r, :].rearrange("p o f -> p (o f)"), ACT.Square,
                                        scale=feats ** -0.5, bias=neg_scaled[0:n, bass.ds(b, 1), r],
                                        accum_out=var[0:n, bass.ds(b, 1), r])
                last.then_inc(var_made, 1)

            def sweep(k):
                for s in range(SLOTS + 1):
                    copy_rows(s, k)
                with act.Fori(1, rounds) as r:
                    for j in range(SLOTS):
                        copy_rows(r * SLOTS + (j + 1), k, j + 1)
                copy_tail(k)

            copy_rows(0, 0)
            for j in range(SLOTS):
                copy_rows(j + 1, 0)
                for q in x_turns[j]:
                    copy_x(q)
            act.wait_ge(plan_made, 1)
            act.wait_ge(hid_made, 1)
            last_turns = Turns(act, rounds)
            with act.Fori(1, rounds) as r:
                turn = Turns(act, r)
                for j in range(SLOTS):
                    copy_rows(r * SLOTS + (j + 1), 0, j + 1)
                    t = TURNS + j // 2
                    if j % 2 == 0:
                        turn.stage(t - 2, square)
                    else:
                        turn.stage(t, relu)

            def brief():
                copy_tail(0)
                square(blocks - 3)
                relu(blocks - 1)
                relu(blocks, 1, hid_bank)
                square(blocks - 2)
                square(blocks - 1)
                square(blocks)

            def in_order(b):
                relu(b)
                square(b)

            def general():
                copy_tail(0)
                last_turns.stage(TURNS - 2, square)
                last_turns.stage(TURNS, relu)
                last_turns.stage(TURNS - 1, square)
                last_turns.stage(TURNS, square)
                late_blocks(act, last_turns, sweep, in_order)
                relu(blocks, 1, hid_bank)
                square(blocks)
            ending(act, last_turns, brief, general)

        @block.vector
        def _(dve):
            V = nc.vector
            count = [0]

            def then(ins):
                count[0] += 1
                ins.then_inc(prep, 1)
                dve.wait_ge(prep, count[0])

            dve.wait_ge(iota_made, 1)
            V.tensor_copy(iota[:, :], iota_int[:, :]).then_inc(iota_made, 1)
            V.tensor_copy(iota_span[:, :], iota_int[:, 0:SPAN]).then_inc(iota_made, 1)
            V.memset(bad[:, :, :], 0.0)
            V.memset(bases[:, :, :], 0)
            then(V.memset(plan[:, :], 0))
            dve.wait_ge(iota_made, 3)
            dve.wait_ge(dst_in, dst_loads)
            V.tensor_reduce(low[:, :], dst_int[:, :, :], AX.X, ALU.min)
            then(V.tensor_reduce(high[:, :], dst_int[:, :, :], AX.X, ALU.max))
            V.tensor_scalar(bad[:, 0, :], low[:, :], 0.0, None, ALU.is_lt)
            V.tensor_scalar(bad[:, 1, :], high[:, :], float(nodes), None, ALU.is_ge)
            V.scalar_tensor_tensor(bad[:, 2, :], low[:, :], float(SPAN), high[:, :], ALU.add, ALU.is_le)
            V.tensor_reduce(group_low[:, :], low[:, :].rearrange("s (g t) -> s g t", g=GROUPS), AX.X, ALU.min)
            then(V.tensor_reduce(group_high[:, :], high[:, :].rearrange("s (g t) -> s g t", g=GROUPS), AX.X, ALU.max))
            then(V.scalar_tensor_tensor(bad[:, 3, 0:GROUPS], group_low[:, :], float(COLS), group_high[:, :], ALU.add, ALU.is_le))
            V.tensor_reduce(bad_count[:, :], bad[:, :, :], AX.XY, ALU.add).then_inc(bad_counted, 1)
            dve.wait_ge(bad_summed, 1)
            then(V.tensor_scalar(good[:, :], t_ps[0][:, 0, 0:1], 0.0, None, ALU.is_equal))
            V.tensor_copy(plan[:, turns + TURNS:turns + TURNS + 1], good[0:1, :])
            V.tensor_scalar(low[:, :], low[:, :], good[0:steps, :], None, ALU.mult)
            then(V.tensor_scalar(group_low[:, :], group_low[:, :], good[0:steps, :], None, ALU.mult))
            V.tensor_tensor(offset[:, :].rearrange("s (g t) -> s g t", g=GROUPS), low[:, :].rearrange("s (g t) -> s g t", g=GROUPS),
                            group_low[:, :].unsqueeze(2).broadcast_to([steps, GROUPS, TILES]), ALU.subtract)
            then(V.tensor_tensor(dst_local[:, :, :], dst_int[:, :, :], low[:, :].unsqueeze(2).broadcast_to([steps, WINS, WIN]), ALU.subtract))
            V.tensor_tensor(row_src[:, :, :, :].rearrange("s g t j -> s (g t) j"),
                            offset[:, :].unsqueeze(2).broadcast_to([steps, WINS, SPAN]),
                            iota[0:steps, 0:SPAN].unsqueeze(1).broadcast_to([steps, WINS, SPAN]), ALU.add).then_inc(local_made, 1)
            for q in range(WINS * RUN // 4):
                dve.wait_ge(ids_turned, q + 1)
                V.tensor_copy(edge_node[:, :, 4 * q:4 * q + 4].rearrange("p s c -> p c s"), t_ps[q % 2][:, :, 0:steps]).then_inc(ids_copied, 1)
            dve.wait_ge(bases_turned, 1)
            V.tensor_copy(bases[:, 1:steps + 1, :].rearrange("p s g -> p g s"), t_ps[1][0:1, 0:GROUPS, 0:steps]).then_inc(bases_made, 1)
            dve.wait_ge(rows_turned, 1)
            V.tensor_copy(row_node[:, :, :].rearrange("p s g -> p g s"), t_ps[0][:, 0:GROUPS, 0:steps]).then_inc(row_node_made, 1)
            dve.wait_ge(bases_made, 1)
            dve.wait_ge(agg_zero, 1)

            def make_hot(s, k, i=None):
                i = (s if i is None else i) % HOTS
                known = isinstance(s, int) and isinstance(k, int)
                if not (known and s < HOTS):
                    dve.wait_ge(level1_done, k * steps + (s - HOTS + 1))
                elif s == 0:
                    dve.wait_ge(ids_copied, WINS * RUN // 4)
                    dve.wait_ge(row_node_made, 1)
                V.tensor_tensor(hot[i][:, :, :],
                                edge_node[:, bass.ds(s, 1), :].rearrange("p o c -> p (o c)").unsqueeze(2).broadcast_to([P, WINS * RUN, SPAN]),
                                iota_span[:, :].unsqueeze(1).broadcast_to([P, WINS * RUN, SPAN]), ALU.is_equal).then_inc(hot_made, 1)
                if not (known and s < HOTS):
                    dve.wait_ge(level2_done, k * steps + (s - HOTS + 1))
                V.tensor_tensor(row_hot[i][:, :, :],
                                row_node[:, bass.ds(s, 1), :].rearrange("p o g -> p (o g)").unsqueeze(2).broadcast_to([P, GROUPS, COLS]),
                                iota[:, 0:COLS].unsqueeze(1).broadcast_to([P, GROUPS, COLS]), ALU.is_equal).then_inc(row_hot_made, 1)

            def add_cols(s, k, at, i=None):
                i = (s if i is None else i) % 2
                last = isinstance(s, int) and s == full
                for g, (mine, other) in enumerate(((added0, added1), (added1, added0))):
                    if last and g == 0:
                        dve.wait_ge(tail_level2_done, k + 1)
                    else:
                        dve.wait_ge(level2_done, k * steps + (s + 1))
                    bank = cols_ps[(i + g) % 2 if last else i]
                    cols = agg_t[:, bass.ds(at[g], COLS)]
                    if not (isinstance(s, int) and isinstance(k, int) and s == 0 and g == 0):
                        dve.wait_ge(other, k * steps + (s + g))
                    V.tensor_tensor(cols, cols, bank[:, g, 0:COLS], ALU.add).then_inc(mine, 1)

            def group_bases(s, n):
                row = bases[:, bass.ds(s + 1, n), :].rearrange("p s g -> p (s g)")
                return ints(dve, row, 0, nodes - 1)

            def residual(b, bank=y_ps):
                n = parts(b)
                dve.wait_ge(y_done, b + 2)
                for r in range(2):
                    zr = z[0:n, bass.ds(b, 1), r, :].rearrange("p o f -> p (o f)")
                    last = V.scalar_tensor_tensor(zr, bank[0:n, r, 0:feats], 1.0, zr, ALU.mult, ALU.add,
                                                  accum_out=total[0:n, bass.ds(b, 1), r])
                last.then_inc(z_made, 1)
                dve.wait_ge(z_made, b + 2)
                V.tensor_scalar(neg_scaled[0:n, bass.ds(b, 1), :], total[0:n, bass.ds(b, 1), :], -feats ** -1.5, None, ALU.mult).then_inc(mean_made, 1)

            def normalise(b):
                n = parts(b)
                dve.wait_ge(neg_made, b + 1)
                dve.wait_ge(rstd_made, b + 1)
                for r in range(2):
                    zr = z[0:n, bass.ds(b, 1), r, :].rearrange("p o f -> p (o f)")
                    last = V.tensor_scalar(zr, zr, neg_mean[0:n, bass.ds(b, 1), r], rstd[0:n, bass.ds(b, 1), r], ALU.add, ALU.mult)
                last.then_inc(normed, 1)

            def sweep(k):
                dve.wait_ge(hot_made, k * steps)
                V.tensor_scalar(iota_span[:, :], iota_span[:, :], float(SPAN), None, ALU.add).then_inc(iota_made, 1)
                dve.wait_ge(iota_made, k + 3)
                at = [k * SPAN, k * SPAN]
                for s in range(HOTS):
                    make_hot(s, k)
                for s in range(1, SLOTS):
                    if s + 2 >= HOTS:
                        make_hot(s + 2, k)
                    add_cols(s - 1, k, at)
                with dve.Fori(1, rounds) as r:
                    for j in range(SLOTS):
                        make_hot(r * SLOTS + (j + 2), k, j + 2)
                        add_cols(r * SLOTS + (j - 1), k, at, j - 1)
                for s in range(full - 2, steps):
                    add_cols(s, k, at)

            for s in range(HOTS):
                make_hot(s, 0)
            then(V.tensor_tensor_scan(low_after[:, :], bases[:, steps:0:-1, 0], bases[:, steps:0:-1, 1],
                                      float(nodes), ALU.min, ALU.min))
            then(V.tensor_copy(whole[:, TURNS:turns], low_after[:, ::-1][:, SLOTS + 1:2 * turns:2]))
            then(V.tensor_scalar(whole[:, TURNS:turns], whole[:, TURNS:turns], shift, None, ALU.arith_shift_right))
            then(V.tensor_scalar(whole_f[:, TURNS:turns], whole[:, TURNS:turns], float(blocks), None, ALU.min))
            then(V.tensor_tensor_scan(begun[:, TURNS:turns], ones[0:1, TURNS:turns], whole_f[:, TURNS:turns], 0.0, ALU.add, ALU.min))
            V.tensor_copy(plan[:, 2 * TURNS:turns + TURNS], begun[:, TURNS:turns]).then_inc(plan_made, 1)

            at = group_bases(0, SLOTS)
            for s in range(1, SLOTS):
                if s + 2 >= HOTS:
                    make_hot(s + 2, 0)
                add_cols(s - 1, 0, at[2 * s - 2:])
            dve.wait_ge(plan_made, 1)
            dve.wait_ge(z_ready, 1)
            last_at = group_bases(full - 2, 3)
            last_turns = Turns(dve, rounds)
            with dve.Fori(1, rounds) as r:
                at = group_bases(r * SLOTS - 1, SLOTS)
                turn = Turns(dve, r)
                for j in range(SLOTS):
                    make_hot(r * SLOTS + (j + 2), 0, j + 2)
                    add_cols(r * SLOTS + (j - 1), 0, at[2 * j:], j - 1)
                    if j % 2 == 0:
                        turn.stage(TURNS + j // 2 - 2, residual)
                    else:
                        turn.stage((j + 1) // 2, normalise)

            def brief():
                add_cols(full - 2, 0, last_at[0:])
                add_cols(full - 1, 0, last_at[2:])
                residual(blocks - 3)
                add_cols(full, 0, last_at[4:])
                normalise(blocks - 4)
                residual(blocks - 2)
                normalise(blocks - 3)
                residual(blocks - 1)
                residual(blocks, y_bank)
                normalise(blocks - 2)
                normalise(blocks - 1)
                normalise(blocks)

            def in_order(b):
                residual(b)
                normalise(b)

            def general():
                add_cols(full - 2, 0, last_at[0:])
                add_cols(full - 1, 0, last_at[2:])
                last_turns.stage(TURNS - 2, residual)
                last_turns.stage(TURNS - 3, normalise)
                add_cols(full, 0, last_at[4:])
                last_turns.stage(TURNS - 1, residual)
                last_turns.stage(TURNS - 2, normalise)
                last_turns.stage(TURNS, residual)
                last_turns.stage(TURNS - 1, normalise)
                last_turns.stage(TURNS, normalise)
                late_blocks(dve, last_turns, sweep, in_order)
                residual(blocks, y_bank)
                normalise(blocks)
            ending(dve, last_turns, brief, general)

        @block.tensor
        def _(pe):
            T = nc.tensor
            pe.wait_ge(ones_made, 1)
            pe.wait_ge(bad_counted, 1)
            T.matmul(t_ps[0][:, 0, 0:1], ones[0:steps, :], bad_count[:, :], start=True, stop=True).then_inc(bad_summed, 1)
            pe.wait_ge(ident_made, 1)
            pe.wait_ge(local_made, 1)
            for q in range(WINS * RUN // 4):
                if q >= 2:
                    pe.wait_ge(ids_copied, q - 1)
                for c in range(4):
                    w, r = divmod(4 * q + c, RUN)
                    last = T.transpose(t_ps[q % 2][:, c, 0:steps], dst_local[:, w, r:WIN:RUN], ident[0:steps, 0:steps])
                last.then_inc(ids_turned, 1)
            pe.wait_ge(ids_copied, WINS * RUN // 4)
            for g in range(GROUPS):
                last = T.transpose(t_ps[1][0:1, g, 0:steps], group_low[:, g:g + 1], ident[0:steps, 0:steps])
            last.then_inc(bases_turned, 1)
            for g in range(GROUPS):
                last = T.transpose(t_ps[0][:, g, 0:steps], row_src[:, g, :, :].rearrange("s t j -> s (t j)"), ident[0:steps, 0:steps])
            last.then_inc(rows_turned, 1)
            pe.wait_ge(w_in, 16 * 7)
            T.matmul(hid_ps[:, 0:1], w1u[:, :], u_col[:, :], start=True, stop=True).then_inc(hid_done, 1)
            T.matmul(y_ps[:, 0, 0:feats], ones[0:1, :], b2_row[:, :], start=True, stop=True).then_inc(y_done, 1)

            turn_banks = [hid_ps[:, :], y_ps[:, :, :].rearrange("p r n -> p (r n)")]

            def turn_x(q):
                if q >= 2:
                    pe.wait_ge(x_copied, q - 1)
                else:
                    pe.wait_ge((hid_made, z_made)[q], 1)
                at = 0
                for b in range(2 * q, min(2 * q + 2, blocks + 1)):
                    n = parts(b)
                    for r in range(2):
                        last = T.transpose(turn_banks[q % 2][:, at:at + n], z[0:n, b, r, :], ident[0:n, 0:n])
                        at += n
                last.then_inc(x_turned, 1)

            def sum_edges(g, i, hot_s, src):
                for e in range(RUN):
                    for t in range(TILES):
                        w = g * TILES + t
                        last = T.matmul(rows_ps[i][t * SPAN:(t + 1) * SPAN, g, 0:feats], hot_s[:, w * RUN + e, :],
                                        src[:, w, e * feats:(e + 1) * feats], start=(e == 0), stop=(e == RUN - 1),
                                        tile_position=(0, t * SPAN))
                return last

            def sum_rows(g, i, n, bank=None):
                bank = cols_ps[i] if bank is None else bank
                return T.matmul(bank[:, g, 0:COLS], rows[i][:, g, :], row_hot[n][:, g, :], start=True, stop=True)

            def level1(s, k, arrived, j=None, i=None):
                i = s if i is None else i
                pe.wait_ge(*arrived)
                pe.wait_ge(hot_made, k * steps + (s + 1))
                if not (isinstance(s, int) and isinstance(k, int) and s < 2):
                    pe.wait_ge(rows_copied, k * steps + (s - 1))
                for g in range(GROUPS):
                    last = sum_edges(g, i % 2, hot[i % HOTS], head if j is None else slots[:, j])
                last.then_inc(level1_done, 1)

            def level2(s, k, i=None):
                i = s if i is None else i
                pe.wait_ge(rows_copied, k * steps + (s + 1))
                pe.wait_ge(row_hot_made, k * steps + (s + 1))
                if not (isinstance(s, int) and isinstance(k, int) and s < 2):
                    pe.wait_ge(added1, k * steps + (s - 1))
                for g in range(GROUPS):
                    last = sum_rows(g, i % 2, i % HOTS)
                last.then_inc(level2_done, 1)

            def tail_level1(k):
                pe.wait_ge(hot_made, k * steps + steps)
                for g, done in enumerate((tail_level1_done, level1_done)):
                    pe.wait_ge(tail_in[g], 16 * (g + 1))
                    pe.wait_ge(rows_copied, k * steps + (full - 1 + g))
                    sum_edges(g, (full + g) % 2, hot[full % HOTS], tail).then_inc(done, 1)

            def tail_level2(k, between=lambda: None):
                i, n = full % 2, full % HOTS
                pe.wait_ge(tail_rows_copied, k + 1)
                pe.wait_ge(row_hot_made, k * steps + steps)
                pe.wait_ge(added1, k * steps + (full - 1))
                sum_rows(0, i, n).then_inc(tail_level2_done, 1)
                between()
                pe.wait_ge(rows_copied, k * steps + steps)
                pe.wait_ge(added1, k * steps + full)
                sum_rows(1, i, n, cols_ps[1 - i]).then_inc(level2_done, 1)

            def product1_x(b, bank=hid_ps):
                n = parts(b)
                T.matmul(bank[:, 0:2 * n], w1x[:, :], x_t[:, bass.ds(b, 1), 0:2 * n].rearrange("f o n -> f (o n)"), start=True, stop=False)

            def product1_agg(b, bank=hid_ps):
                n = parts(b)
                T.matmul(bank[:, 0:2 * n], w1a[:, :], agg_t[:, bass.ds(b * pair, 2 * n)], start=False, stop=True).then_inc(hid_done, 1)

            def product1(b):
                pe.wait_ge(hid_made, b + 1)
                product1_x(b)
                product1_agg(b)

            def product2(b, n=0, bank=y_ps):
                m = parts(b)
                pe.wait_ge(hid_made, b + 2)
                if n == 0:
                    pe.wait_ge(z_made, b + 1)
                for r in range(2):
                    last = T.matmul(bank[0:m, r, 0:feats], hid[n][:, r:2 * m:2], w2_sb[:, :], start=True, stop=True)
                last.then_inc(y_done, 1)

            def arrived(j, r, k):
                return edges_in[j], 16 * (k * rounds + (r + 1))

            def first_steps(k, between=lambda j: None):
                level1(0, k, (head_in, 16))
                for j in range(SLOTS):
                    level1(j + 1, k, arrived(j, 0, k), j)
                    level2(j, k)
                    between(j)

            def sweep(k):
                first_steps(k)
                with pe.Fori(1, rounds) as r:
                    for j in range(SLOTS):
                        level1(r * SLOTS + (j + 1), k, arrived(j, r, k), j, j + 1)
                        level2(r * SLOTS + j, k, j)
                level2(full - 1, k)
                tail_level1(k)
                tail_level2(k)

            pe.wait_ge(x_in, 16 * 3)
            first_steps(0, lambda j: [turn_x(q) for q in x_turns[j]])
            pe.wait_ge(plan_made, 1)
            pe.wait_ge(x_copied, blocks // 2 + 1)
            last_turns = Turns(pe, rounds)
            with pe.Fori(1, rounds) as r:
                turn = Turns(pe, r)
                for j in range(SLOTS):
                    t = TURNS + j // 2
                    level1(r * SLOTS + (j + 1), 0, arrived(j, r, 0), j, j + 1)
                    level2(r * SLOTS + j, 0, j)
                    if j % 2 == 0:
                        turn.stage(t - 1, product2)
                    else:
                        pe.wait_ge(added1, r * SLOTS + j)
                        turn.stage(t, product1)

            def product1_before_tail(b):
                pe.wait_ge(added1, full)
                product1(b)

            def brief():
                level2(full - 1, 0)
                tail_level1(0)
                tail_level2(0, lambda: product1_before_tail(blocks - 1))
                product2(blocks - 2)
                product1_x(blocks, hid_bank)
                pe.wait_ge(added1, steps)
                product1_agg(blocks, hid_bank)
                product2(blocks - 1)
                product2(blocks, 1, y_bank)

            def in_order(b):
                product1(b)
                product2(b)

            def general():
                level2(full - 1, 0)
                tail_level1(0)
                tail_level2(0, lambda: last_turns.stage(TURNS, product1_before_tail))
                last_turns.stage(TURNS - 1, product2)
                last_turns.stage(TURNS, product2)
                pe.wait_ge(added1, steps)
                late_blocks(pe, last_turns, sweep, in_order)
                product1_x(blocks, hid_bank)
                product1_agg(blocks, hid_bank)
                product2(blocks, 1, y_bank)
            ending(pe, last_turns, brief, general)


_USED = ["x", "dst", "edge_attr_128", "L0_gnn_u", "L0_gnn_W1", "L0_gnn_b1", "L0_gnn_W2", "L0_gnn_b2"]


def kernel(**inputs):
    import numpy as np
    import concourse.bacc as bacc
    from concourse.bass_utils import run_bass_kernel_spmd

    nc = bacc.Bacc("TRN2", target_bir_lowering=False, num_devices=1)
    arrays, args = {}, []
    for name in _USED:
        a = np.ascontiguousarray(inputs[name])
        arrays[f"in_{name}"] = a
        args.append(nc.dram_tensor(f"in_{name}", a.shape, mybir.dt.from_np(a.dtype), kind="ExternalInput").ap())
    shape = np.asarray(inputs["x"]).shape
    args.append(nc.dram_tensor("out_0", shape, F32, kind="ExternalOutput").ap())
    residual_gnn_layer(nc, *args)
    done = run_bass_kernel_spmd(nc, [arrays], core_ids=[0])
    return done.results[0]["out_0"]
```
